# Optimizing a Trainium2 kernel written in Bass

```python
import numpy as np
import jax
import jax.numpy as jnp

def _softmax(x, axis=-1):
    return jax.nn.softmax(x, axis=axis)

def _gelu(x):
    return jax.nn.gelu(x, approximate=True)

def _silu(x):
    return jax.nn.silu(x)

def _sigmoid(x):
    return jax.nn.sigmoid(x)

def _layernorm(x, axis=-1, eps=1e-05):
    m = jnp.mean(x, axis=axis, keepdims=True)
    v = jnp.var(x, axis=axis, keepdims=True)
    return (x - m) / jnp.sqrt(v + eps)

def _scatter_add(tgt, idx, src, axis=0):
    return tgt.at[idx].add(src)

def _segment_sum(src, seg, n):
    return jax.ops.segment_sum(src, seg, n)
kernel_name = 'mk_perceiver_d1_seqx_r4_e1e522'

def setup_inputs(seed: int=0):
    np.random.seed(seed)
    _w = jnp.asarray

    def _rec_inputs():
        import jax
        import jax.numpy as jnp
        _rk = jax.random.key(seed)
        x = -0.0003929 + 0.9999 * jax.random.normal(jax.random.fold_in(_rk, 1), (64, 64, 256), jnp.float32)
        _lenS = 64 - jax.random.randint(jax.random.fold_in(_rk, 7), (64,), 0, max(1, 64 // 4) + 1, jnp.int32)
        _lenS2 = 256 - jax.random.randint(jax.random.fold_in(_rk, 8), (64,), 0, max(1, 256 // 4) + 1, jnp.int32)
        _ctx_768P = jax.random.normal(jax.random.fold_in(_rk, 11), (64, 16, 192), jnp.float32)
        _ctx_768c = jax.random.dirichlet(jax.random.fold_in(_rk, 511), 0.3 * jnp.ones((16,), jnp.float32), (64, 256))
        _ctx_768t = jnp.einsum('bsk,bkd->bsd', _ctx_768c, _ctx_768P)
        _ctx_768t = _ctx_768t * jax.lax.rsqrt(jnp.mean(jnp.square(_ctx_768t)) + 1e-12) * 0.953939
        ctx_768 = -7.36909e-05 + 0.999899 * (_ctx_768t + 0.3 * jax.random.normal(jax.random.fold_in(_rk, 611), (64, 256, 192), jnp.float32))
        return (x, ctx_768)
    x, ctx_768 = _rec_inputs()

    def _L0_xattn_setup():
        import jax, jax.numpy as jnp
        import numpy as np
        EPS = 1e-08
        key = jax.random.key(seed)
        kv, kt, k1, k2, k3, k4 = jax.random.split(key, 6)
        B, S = (16, 256)
        VD, TD, H = (256, 192, 128)
        visual_features = jax.random.normal(kv, (B, S, VD), dtype=jnp.float32)
        text_features = jax.random.normal(kt, (B, S, TD), dtype=jnp.float32)
        Wv = jax.random.normal(k1, (H, VD), dtype=jnp.float32) * (1.0 / np.sqrt(VD))
        bv = jax.random.normal(k2, (H,), dtype=jnp.float32) * 0.01
        Wt = jax.random.normal(k3, (H, TD), dtype=jnp.float32) * (1.0 / np.sqrt(TD))
        bt = jax.random.normal(k4, (H,), dtype=jnp.float32) * 0.01
        return {'visual_features': visual_features, 'text_features': text_features, 'Wv': Wv, 'bv': bv, 'Wt': Wt, 'bt': bt}
    _L0_xattn_all = _L0_xattn_setup()
    _L0_xattn_in = {k: v for k, v in _L0_xattn_all.items() if k in ('Wv', 'bv', 'Wt', 'bt')}
    del _L0_xattn_all

    def _L0_attn_setup():
        import jax, jax.numpy as jnp
        import numpy as np
        D_MODEL = 256
        NUM_HEADS = 16
        HEAD_DIM = D_MODEL // NUM_HEADS
        B, S = (2, 512)
        EPS = 1e-08
        key = jax.random.key(seed)
        ks = jax.random.split(key, 9)
        sc = 1.0 / np.sqrt(D_MODEL)
        return {'x': jax.random.normal(ks[0], (B, S, D_MODEL), jnp.float32), 'wq': jax.random.normal(ks[1], (D_MODEL, D_MODEL), jnp.float32) * sc, 'bq': jax.random.normal(ks[2], (D_MODEL,), jnp.float32) * 0.01, 'wk': jax.random.normal(ks[3], (D_MODEL, D_MODEL), jnp.float32) * sc, 'bk': jax.random.normal(ks[4], (D_MODEL,), jnp.float32) * 0.01, 'wv': jax.random.normal(ks[5], (D_MODEL, D_MODEL), jnp.float32) * sc, 'bv': jax.random.normal(ks[6], (D_MODEL,), jnp.float32) * 0.01, 'wo': jax.random.normal(ks[7], (D_MODEL, D_MODEL), jnp.float32) * sc, 'bo': jax.random.normal(ks[8], (D_MODEL,), jnp.float32) * 0.01}
    _L0_attn_all = _L0_attn_setup()
    _L0_attn_in = {k: v for k, v in _L0_attn_all.items() if k in ('wq', 'bq', 'wk', 'bk', 'wv', 'bv', 'wo', 'bo')}
    del _L0_attn_all

    def _L0_ffn_setup():
        import jax, jax.numpy as jnp
        import numpy as np
        B, S, D, E, F = (2, 512, 256, 14, 512)
        key = jax.random.key(seed)
        k = jax.random.split(key, 4)
        h = jax.random.normal(k[0], (B, S, D), dtype=jnp.float32)
        router_w = jax.random.normal(k[1], (D, E), dtype=jnp.float32) * 0.02
        w1 = jax.random.uniform(k[2], (E, D, F), dtype=jnp.float32, minval=-1.0, maxval=1.0) * float(np.sqrt(6.0 / D))
        w2 = jax.random.uniform(k[3], (E, F, D), dtype=jnp.float32, minval=-1.0, maxval=1.0) * float(np.sqrt(6.0 / F))
        b1 = jnp.zeros((E, F), dtype=jnp.float32)
        b2 = jnp.zeros((E, D), dtype=jnp.float32)
        return {'h': h, 'router_w': router_w, 'w1': w1, 'b1': b1, 'w2': w2, 'b2': b2}
    _L0_ffn_all = _L0_ffn_setup()
    _L0_ffn_in = {k: v for k, v in _L0_ffn_all.items() if k in ('router_w', 'w1', 'b1', 'w2', 'b2')}
    del _L0_ffn_all
    return {'x': x, 'ctx_768': ctx_768, 'L0_xattn_Wv': _L0_xattn_in['Wv'], 'L0_xattn_bv': _L0_xattn_in['bv'], 'L0_xattn_Wt': _L0_xattn_in['Wt'], 'L0_xattn_bt': _L0_xattn_in['bt'], 'L0_attn_wq': _L0_attn_in['wq'], 'L0_attn_bq': _L0_attn_in['bq'], 'L0_attn_wk': _L0_attn_in['wk'], 'L0_attn_bk': _L0_attn_in['bk'], 'L0_attn_wv': _L0_attn_in['wv'], 'L0_attn_bv': _L0_attn_in['bv'], 'L0_attn_wo': _L0_attn_in['wo'], 'L0_attn_bo': _L0_attn_in['bo'], 'L0_ffn_router_w': _L0_ffn_in['router_w'], 'L0_ffn_w1': _L0_ffn_in['w1'], 'L0_ffn_b1': _L0_ffn_in['b1'], 'L0_ffn_w2': _L0_ffn_in['w2'], 'L0_ffn_b2': _L0_ffn_in['b2']}

def reference(x, ctx_768, L0_xattn_Wv, L0_xattn_bv, L0_xattn_Wt, L0_xattn_bt, L0_attn_wq, L0_attn_bq, L0_attn_wk, L0_attn_bk, L0_attn_wv, L0_attn_bv, L0_attn_wo, L0_attn_bo, L0_ffn_router_w, L0_ffn_w1, L0_ffn_b1, L0_ffn_w2, L0_ffn_b2):
    import jax
    import jax.numpy as jnp

    def _L0_xattn_ref(visual_features, text_features, Wv, bv, Wt, bt):
        import jax, jax.numpy as jnp
        import numpy as np
        EPS = 1e-08
        v = jnp.einsum('bsd,hd->bsh', visual_features, Wv) + bv
        t = jnp.einsum('bsd,hd->bsh', text_features, Wt) + bt
        dots = jnp.einsum('bih,bjh->bij', v, t)
        vn = jnp.linalg.norm(v, axis=-1)
        tn = jnp.linalg.norm(t, axis=-1)
        denom = jnp.maximum(vn[:, :, None] * tn[:, None, :], EPS)
        return dots / denom

    def _L0_attn_ref(x, wq, bq, wk, bk, wv, bv, wo, bo):
        import jax, jax.numpy as jnp
        import numpy as np
        D_MODEL = 256
        NUM_HEADS = 16
        HEAD_DIM = D_MODEL // NUM_HEADS
        B, S = (2, 512)
        EPS = 1e-08
        b, s, d = x.shape
        h, hd = (NUM_HEADS, HEAD_DIM)

        def proj(w, bias):
            return (jnp.einsum('bsd,ed->bse', x, w) + bias).reshape(b, s, h, hd).transpose(0, 2, 1, 3)
        q = proj(wq, bq)
        k = proj(wk, bk)
        v = proj(wv, bv)
        scores = jnp.einsum('bhqd,bhkd->bhqk', q, k) / np.sqrt(hd)
        attn = jax.nn.softmax(scores, axis=-1)
        o = jnp.einsum('bhqk,bhkd->bhqd', attn, v)
        v_norm_sq = jnp.sum(v * v, axis=-1, keepdims=True)
        align = jnp.sum(o * v, axis=-1, keepdims=True) / (v_norm_sq + EPS)
        o = o - align * v
        o = o.transpose(0, 2, 1, 3).reshape(b, s, d)
        return jnp.einsum('bsd,ed->bse', o, wo) + bo

    def _L0_ffn_ref(h, router_w, w1, b1, w2, b2):
        import jax, jax.numpy as jnp
        import numpy as np
        B, S, D, E, F = (2, 512, 256, 14, 512)
        Bb, Ss, Dd = h.shape
        x = h.reshape(-1, Dd)
        logits = x @ router_w
        assignments = jnp.argmax(logits, axis=-1)
        probs = jax.nn.softmax(logits, axis=-1)
        weights = jnp.take_along_axis(probs, assignments[:, None], axis=1)[:, 0]
        hid = jnp.einsum('nd,edf->nef', x, w1) + b1
        hid = jax.nn.gelu(hid, approximate=False)
        all_out = jnp.einsum('nef,efd->ned', hid, w2) + b2
        sel = jnp.take_along_axis(all_out, assignments[:, None, None], axis=1)[:, 0, :]
        moe_out = (sel * weights[:, None]).reshape(Bb, Ss, Dd)
        return moe_out
    x = x + _L0_xattn_ref(_layernorm(x, axis=-1), ctx_768, L0_xattn_Wv, L0_xattn_bv, L0_xattn_Wt, L0_xattn_bt)
    x = x + _L0_attn_ref(_layernorm(x, axis=-1), L0_attn_wq, L0_attn_bq, L0_attn_wk, L0_attn_bk, L0_attn_wv, L0_attn_bv, L0_attn_wo, L0_attn_bo)
    x = x + _L0_ffn_ref(_layernorm(x, axis=-1), L0_ffn_router_w, L0_ffn_w1, L0_ffn_b1, L0_ffn_w2, L0_ffn_b2)
    return x

_drawn_inputs = setup_inputs


def setup_inputs(seed=0):
    import zlib

    import numpy as np

    out = dict(_drawn_inputs(seed))
    spreads = {'L0_ffn_b1': (0.0, 0.68), 'L0_ffn_b2': (0.0, 0.676)}
    factors = {'L0_xattn_bv': 21.271,
     'L0_xattn_bt': 46.176,
     'L0_attn_bq': 8.0,
     'L0_attn_bk': 64.0,
     'L0_attn_bv': 3.406,
     'L0_attn_bo': 2.911}
    for name, (base, spread) in spreads.items():
        noise = np.random.default_rng([zlib.crc32(name.encode()), seed]).standard_normal(out[name].shape)
        drawn = base * np.exp(spread * noise) if base else spread * noise
        out[name] = jnp.asarray(drawn.astype(out[name].dtype))
    for name, factor in factors.items():
        out[name] = (out[name] * factor).astype(out[name].dtype)
    return out
```

```python
from contextlib import ExitStack

import numpy as np

import concourse.bass as bass
from concourse import mybir

F32 = mybir.dt.float32
BF16 = mybir.dt.bfloat16
U32 = mybir.dt.uint32
I32 = mybir.dt.int32
ALU = mybir.AluOpType
ACT = mybir.ActivationFunctionType
AX = mybir.AxisListType

P = 128
B, S, D = 64, 64, 256
SC, DC, H = 256, 192, 128
NH, HD = 16, 16
E, F = 14, 512
NTOK = B * S
NT = NTOK // P
CK = DC // 2
KC = D // P
FC = F // P
HC = P // HD
NPAIR = NH // 2
VW = 2 * (HD + 1)
EW = KC * F + FC * D
NSLOT = NTOK // P + E - 1
REGION = NTOK + P
REC = 264
R_RSTD, R_MEAN, R_VAR, R_PROB, R_TOK = D, D + 1, D + 2, D + 3, D + 4
NOWHERE = 1 << 20
LN_EPS, ATT_EPS, COS_EPS = 1e-5, 1e-8, 1e-8
LO, HI = 8, 28
TURN = 4


def need(engine, semaphore, value, most=None):
    if isinstance(value, int):
        if value <= 0:
            return
        if most is not None:
            value = min(value, most)
    engine.wait_ge(semaphore, value)


def run_steps(engine, step, first, last, lo=LO, hi=HI, turn=TURN):
    for i in range(first, lo):
        step(i, i % turn)
    with engine.Fori(0, (hi - lo) // turn) as n:
        for k in range(turn):
            step(n * turn + (lo + k), (lo + k) % turn)
    for i in range(hi, last):
        step(i, i % turn)


def live(t, count=NT):
    return not isinstance(t, int) or 0 <= t < count


def arrivals(t, slot, ring, each):
    if isinstance(t, int):
        return each * (t // ring + 1)
    return (t - slot) * (each // ring) + each


def build(nc, x, ctxT, wvT, wtT, xbv, xbt, wqT, wkT, avT, woT, bq, bk, bv, bo, routerT, weights, b1T, b2, out):
    routed = nc.dram_tensor("routed", ((E + 1) * REGION, REC), F32).ap()
    ctx = ExitStack()
    with ctx:
        def sb(name, shape, dtype=F32):
            return ctx.enter_context(nc.sbuf_tensor(name, shape, dtype))

        def sem(name):
            return ctx.enter_context(nc.semaphore(name))

        W = sb("W", [P, E * EW])
        ctx_in_sb = W[:, 0:2 * EW].rearrange("p (s c j) -> p s c j", s=4, c=2)
        tT = W[:, 2 * EW:2 * EW + 2 * F].rearrange("p (s j) -> p s j", s=2)
        tsq = W[:, 2 * EW + 2 * F:3 * EW].rearrange("p (s j) -> p s j", s=2)
        early = W[:, 3 * EW:3 * EW + 18 * P]
        vT, vsq, vnorm = (early[:, n * D:(n + 1) * D].rearrange("p (s j) -> p s j", s=2) for n in range(3))
        norm, rnorm, cos = (early[:, 6 * P + n * 2 * SC:6 * P + (n + 1) * 2 * SC].rearrange("p (s j) -> p s j", s=2)
                            for n in range(3))
        tok = W[:, (E - 4) * EW:E * EW]

        def rows(t):
            return tok[:, bass.ds(t * D, D)]

        wv_s = sb("wv_s", [P, KC, H])
        wt_s = sb("wt_s", [CK, 2, H])
        wq_s = sb("wq_s", [P, KC, D])
        wk_s = sb("wk_s", [P, KC, D])
        av_s = sb("av_s", [P, KC, D])
        wo_s = sb("wo_s", [P, KC, D])
        rt_s = sb("rt_s", [P, KC, E])
        xbv_s = sb("xbv_s", [P, 1])
        xbt_s = sb("xbt_s", [P, 1])
        bq_s = sb("bq_s", [P, KC])
        bk_s = sb("bk_s", [P, KC])
        bv_s = sb("bv_s", [P, D])
        bo_s = sb("bo_s", [P, D])
        b1_s = sb("b1_s", [P, E * FC])
        ident = sb("ident", [P, P])
        ones = sb("ones", [P, P])
        ones16 = sb("ones16", [P, P], BF16)
        before16 = sb("before16", [P, P], BF16)
        mhalf = sb("mhalf", [P, 1])
        eps = sb("eps", [P, 1])
        zero_u = sb("zero_u", [P, 1], U32)
        token_of = sb("token_of", [P, 4, 1], U32)
        iota_e = sb("iota_e", [P, E])
        token_ids = sb("token_ids", [P, NT], U32)
        slot_no = sb("slot_no", [1, NSLOT, E])
        region0 = sb("region0", [1, E])
        pad_rec = sb("pad_rec", [P, REC])

        arena = sb("arena", [P, 10560])
        kd = arena[:, 0:4096].rearrange("p (s c b j) -> p s c b j", s=2, c=KC, b=2)
        prob = arena[:, 4096:6144].rearrange("p (s j) -> p s j", s=2)
        probT = arena[:, 6144:8192].rearrange("p (s j) -> p s j", s=2)
        vd = arena[:, 8192:8192 + 4 * NPAIR * VW].rearrange("p (s b n j) -> p s b n j", s=2, b=2, n=NPAIR)
        hid = arena[:, 0:1024].rearrange("p (s j) -> p s j", s=2)
        hidT = arena[:, 1024:2048].rearrange("p (s j) -> p s j", s=2)
        xg = arena[:, 2048:2560].rearrange("p (s j) -> p s j", s=2)
        xgT = arena[:, 2560:3072].rearrange("p (s j) -> p s j", s=2)
        ysum = arena[:, 3072:3584].rearrange("p (s j) -> p s j", s=2)
        yout = arena[:, 3584:4608].rearrange("p (s j) -> p s j", s=4)
        slot_rec = arena[:, 4608:4608 + 4 * REC].rearrange("p (s j) -> p s j", s=4)
        b2_s = arena[:, 5664:5664 + E * D]
        passed, started = (arena[0:1, 9248 + n * 640:9248 + n * 640 + NSLOT * E].rearrange("p (n e) -> p n e", e=E)
                           for n in range(2))

        xn = sb("xn", [P, 2, D])
        xnT = sb("xnT", [P, 2, D])
        stats = sb("stats", [P, 2, 6])
        mv = sb("mv", [P, 2, 2])
        vareps = sb("vareps", [P, 2, 1])
        rstd = sb("rstd", [P, 2, 1])

        qT = sb("qT", [P, 2, KC * P])
        kT = sb("kT", [P, 2, KC * P])
        v_s = sb("v_s", [P, 4, D])
        v_swap = sb("v_swap", [P, 2, D])
        vv = sb("vv", [P, D])
        vvsum = sb("vvsum", [P, NH])
        rvv = sb("rvv", [P, 4, NH])
        smax = sb("smax", [P, NH])
        rsum = sb("rsum", [P, NH])
        o_n = sb("o_n", [P, D])
        ov = sb("ov", [P, D])
        dot = sb("dot", [P, NH])
        coef = sb("coef", [P, NH])
        along = sb("along", [P, D])
        o_f = sb("o_f", [P, 2, D])
        oT = sb("oT", [P, 2, D])
        stats3 = sb("stats3", [P, 6])
        vareps3 = sb("vareps3", [P, 1])
        x3n = sb("x3n", [P, 2, D])
        x3T = sb("x3T", [P, 2, D])
        rec = sb("rec", [P, 4, REC])
        logit = sb("logit", [P, 2, E])
        top8 = sb("top8", [P, 8])
        arg8 = sb("arg8", [P, 8], U32)
        argf = sb("argf", [P, 2, 1])
        ntop = sb("ntop", [P, 2, 1])
        onehot = sb("onehot", [P, 2, E], BF16)
        earlier = sb("earlier", [P, 2, E], BF16)
        expl = sb("expl", [P, E])
        lsum = sb("lsum", [P, 2, 1])
        ranked = sb("ranked", [P, E])
        rank = sb("rank", [P, 1])
        posf = sb("posf", [P, 1])
        pos = sb("pos", [P, 4, 1], U32)
        counts = sb("counts", [1, E])
        plan_i = sb("plan_i", [1, E], I32)
        tiles_of = sb("tiles_of", [1, E])
        ends = sb("ends", [1, 2, E])
        slot_e = sb("slot_e", [1, NSLOT])
        slot_s = sb("slot_s", [1, NSLOT])
        slot_b = sb("slot_b", [1, NSLOT])
        expert_tab = sb("expert_tab", [1, NSLOT], I32)
        base_tab = sb("base_tab", [1, NSLOT], I32)
        padf = sb("padf", [1, E])
        pad_tab = sb("pad_tab", [1, E], I32)

        psum = ctx.enter_context(nc.psum_tensor("psum", [P, 8 * 512], F32))

        def bank(n, width=512):
            return psum[:, n * 512:n * 512 + width]

        x_in = [sem(f"x_in{n}") for n in range(4)]
        ctx_in = [sem(f"ctx_in{n}") for n in range(4)]
        kd_in = [sem(f"kd_in{n}") for n in range(2)]
        swap_in = [sem(f"swap_in{n}") for n in range(2)]
        rec_out = [sem(f"rec_out{n}") for n in range(4)]
        rec_in = [sem(f"rec_in{n}") for n in range(4)]
        y_out = [sem(f"y_out{n}") for n in range(4)]
        names = """
            a_consts_in consts_in zeroed consts_made vd_ones weights_in b2_in pads_out
            a_stats_raw a_stats a_vareps a_rstd a_xn a_xT_psum a_xT t_psum t_sbuf v_psum v_sbuf
            vnorm_psum vnorm_sbuf norms_psum dots_psum norms_sbuf norms_inv cos_sbuf tok_sum
            stats_raw stats_ok vareps_ok rstd_ok xn_ok xT_psum xT_ok qk_psum k_ok q_ok
            val_psum val_ok vv_ok vvsum_raw rvv_raw rvv_ok vd_ok s_psum smax_ok centred exp_ok pT_psum pT_ok
            o_psum rsum_ok on_ok ov_ok dot_ok coef_ok along_ok of_ok oT_psum oT_ok wo_psum x3_ok
            bo_added stats3_raw stats3_ok vareps3_ok rstd3_ok x3n_ok x3T_psum x3T_ok l_psum logit_ok
            top_ok arg_ok argf_ok ntop_ok onehot_ok earlier_ok lsum_ok token_ok rank_psum ranked_ok rank_ok
            posf_ok pos_ok count_psum plan plan_ok
            g_token g_xg g_xT_psum g_xT g_h_psum g_h g_hT_psum g_hT g_y_psum g_ysum g_y
        """.split()
        s = {n: sem(n) for n in names}

        block = ctx.enter_context(nc.Block())

        @block.sync
        def _(sp):
            first = [(wv_s[:, :, :], wvT), (wt_s[:, :, :], wtT), (xbv_s[:, :], xbv), (xbt_s[:, :], xbt)]
            rest = [(wq_s[:, :, :], wqT), (wk_s[:, :, :], wkT), (av_s[:, :, :], avT), (wo_s[:, :, :], woT),
                    (rt_s[:, :, :], routerT), (bq_s[:, :], bq), (bk_s[:, :], bk), (b1_s[:, :], b1T),
                    (bv_s[:, :], bv.broadcast_to([P, D])), (bo_s[:, :], bo.broadcast_to([P, D]))]
            for to, source in first:
                sp.dma_start(to, source).then_inc(s["a_consts_in"], 16)

            def load_tokens(i, k):
                if isinstance(i, int) and i == 4:
                    for to, source in rest:
                        sp.dma_start(to, source).then_inc(s["consts_in"], 16)
                need(sp, x_in[k], arrivals(i - 4, k, 4, 16))
                sp.dma_start(rows(i), x[bass.ds(i * P, P), :]).then_inc(x_in[k], 16)
                need(sp, s["t_psum"], i - 3)
                sp.dma_start(ctx_in_sb[0:CK, k], ctxT[bass.ds(i, 1)].rearrange("o p c j -> (o p) c j"))\
                    .then_inc(ctx_in[k], 16)
            run_steps(sp, load_tokens, 0, NT)

            sp.wait_ge(s["zeroed"], 5)
            sp.wait_ge(s["cos_sbuf"], NT)

            def load_expert(e):
                sp.dma_start(W[:, e * EW:(e + 1) * EW].rearrange("p (h j) -> p h j", h=2),
                             weights[2 * e:2 * e + 2].rearrange("h p j -> p h j")).then_inc(s["weights_in"], 16)

            def attention_moves(i, k):
                p = k % 2
                if live(i):
                    need(sp, s["s_psum"], i - 1)
                if not isinstance(i, int):
                    half = i - LO
                    sp.dma_start(W[:, bass.ds(half * (EW // 2), EW // 2)],
                                 weights[bass.ds(half, 1)].rearrange("o p j -> (o p) j")).then_inc(s["weights_in"], 16)
                elif i == HI:
                    sp.wait_ge(s["x3_ok"], 16)
                    load_expert(E - 4)
                    load_expert(E - 3)
                elif i == HI + 2:
                    sp.wait_ge(s["x3_ok"], 24)
                    load_expert(E - 2)
                if live(i):
                    need(sp, s["k_ok"], i + 1)
                    for h in range(HC):
                        r = slice(h * HD, (h + 1) * HD)
                        sp.dma_start(kd[r, p, :, :, h * S:(h + 1) * S].rearrange("p c b j -> p (c b) j"),
                                     kT[r, p, :].rearrange("p (n j) -> p n j", j=S)).then_inc(kd_in[p], 16)
                    need(sp, s["val_ok"], i + 1)
                    need(sp, s["vd_ok"], i - 1)
                    for b in range(2):
                        sp.dma_start(v_swap[(1 - b) * S:(2 - b) * S, p, :], v_s[b * S:(b + 1) * S, k, :])\
                            .then_inc(swap_in[p], 16)
            run_steps(sp, attention_moves, 0, NT)
            sp.wait_ge(s["x3_ok"], NT)
            load_expert(E - 1)
            sp.dma_start(b2_s, b2.broadcast_to([P, E * D])).then_inc(s["b2_in"], 16)

            sp.wait_ge(s["plan_ok"], 1)
            for e in range(E):
                at = sp.value_load(pad_tab[0:1, e:e + 1], min_val=e * REGION, max_val=e * REGION + NTOK)
                sp.dma_start(routed[bass.ds(at, P), :], pad_rec[:, :]).then_inc(s["pads_out"], 16)
            sp.dma_start(routed[E * REGION:E * REGION + P, :], pad_rec[:, :]).then_inc(s["pads_out"], 16)
            sp.wait_ge(s["pads_out"], 16 * (E + 1))
            for r in range(4):
                sp.wait_ge(rec_out[r], arrivals(NT - 4 + r, r, 4, 16))

            def load_slot(i, k):
                need(sp, s["g_y"], i - 3)
                need(sp, s["g_token"], i - 3)
                at = sp.value_load(base_tab[0:1, bass.ds(i, 1)], min_val=0, max_val=E * REGION)
                sp.dma_start(slot_rec[:, k, :], routed[bass.ds(at, P), :]).then_inc(rec_in[k], 16)
            run_steps(sp, load_slot, 0, NSLOT, 8, 40)
            for r in range(4):
                last = NSLOT - 1 - (NSLOT - 1 - r) % 4
                sp.wait_ge(y_out[r], arrivals(last, r, 4, 16))

        @block.gpsimd
        def _(pool):
            for tile, value in ((ident, 0.0), (before16, 1.0), (arena, 0.0), (rec, 0.0), (pad_rec, 0.0)):
                pool.memset(tile[:], value).then_inc(s["zeroed"], 1)
            for tile, value in ((ones, 1.0), (mhalf, -0.5), (eps, LN_EPS), (zero_u, 0), (ones16, 1.0), (earlier, 0.0)):
                pool.memset(tile[:], value).then_inc(s["consts_made"], 1)
            pool.wait_ge(s["zeroed"], 5)
            pool.affine_select(out=ident[:, :], in_=ident[:, :], compare_op=ALU.not_equal, fill=1.0, base=0,
                               pattern=[[-1, P]], channel_multiplier=1).then_inc(s["consts_made"], 1)
            pool.affine_select(out=before16[:, :], in_=before16[:, :], compare_op=ALU.is_gt, fill=0.0, base=0,
                               pattern=[[1, P]], channel_multiplier=-1).then_inc(s["consts_made"], 1)
            pool.iota(iota_e[:, :], [[1, E]], base=0, channel_multiplier=0,
                      allow_small_or_imprecise_dtypes=True).then_inc(s["consts_made"], 1)
            pool.iota(token_ids[:, :], [[P, NT]], base=0, channel_multiplier=1).then_inc(s["consts_made"], 1)
            pool.iota(slot_no[:, :, :], [[1, NSLOT], [0, E]], base=0, channel_multiplier=0,
                      allow_small_or_imprecise_dtypes=True).then_inc(s["consts_made"], 1)
            pool.iota(region0[:, :], [[REGION, E]], base=0, channel_multiplier=0,
                      allow_small_or_imprecise_dtypes=True).then_inc(s["consts_made"], 1)
            pool.iota(pad_rec[:, R_TOK:R_TOK + 1].bitcast(U32), [[0, 1]], base=NOWHERE, channel_multiplier=0)\
                .then_inc(s["consts_made"], 1)
            pool.wait_ge(s["consts_made"], 13)

            def context_step(i, k):
                t, p = i + 2, k % 2
                if live(t):
                    need(pool, s["a_stats"], t + 1)
                    pool.tensor_tensor(vareps[:, p], mv[:, p, 1:2], eps[:, :], ALU.add).then_inc(s["a_vareps"], 1)
                    need(pool, s["a_vareps"], t + 1)
                    need(pool, s["a_xn"], t - 1)
                    pool.tensor_tensor(rstd[:, p], vareps[:, p], mhalf[:, :], ALU.pow).then_inc(s["a_rstd"], 1)
                u, q = i - 1, (k - 1) % 2
                if live(u):
                    need(pool, s["cos_sbuf"], u + 1)
                    pool.tensor_tensor(rows(u), rows(u), cos[:, q, :], ALU.add).then_inc(s["tok_sum"], 1)
            run_steps(pool, context_step, -2, NT + 1)

            def attention_step(i, k):
                y, w, x, n = i - 3, i - 4, i - 6, i + 2
                if live(x):
                    need(pool, s["pos_ok"], x + 1)
                    need(pool, s["token_ok"], x + 1)
                    need(pool, s["rstd3_ok"], x + 1)
                if live(w):
                    r = (k - 4) % 4
                    need(pool, s["stats3_ok"], w + 1)
                    pool.tensor_tensor(vareps3[:, :], rec[:, r, R_VAR:R_VAR + 1], eps[:, :], ALU.add)\
                        .then_inc(s["vareps3_ok"], 1)
                    pool.tensor_copy(rec[:, r, R_TOK:R_TOK + 1].bitcast(U32), token_ids[:, bass.ds(w, 1)])\
                        .then_inc(s["token_ok"], 1)
                    need(pool, s["vareps3_ok"], w + 1)
                    pool.tensor_tensor(rec[:, r, R_RSTD:R_RSTD + 1], vareps3[:, :], mhalf[:, :], ALU.pow)\
                        .then_inc(s["rstd3_ok"], 1)
                if live(y):
                    need(pool, s["on_ok"], y + 1)
                    pool.tensor_tensor(ov[:, :], o_n[:, :], v_s[:, (k - 3) % 4, :], ALU.mult).then_inc(s["ov_ok"], 1)
                if live(i):
                    need(pool, s["xn_ok"], i + 1)
                    pool.tensor_tensor(rows(i), rows(i), bo_s[:, :], ALU.add).then_inc(s["bo_added"], 1)
                if live(y):
                    need(pool, s["coef_ok"], y + 1)
                    v_y = v_s[:, (k - 3) % 4, :].rearrange("p (h d) -> p h d", h=NH)
                    pool.tensor_tensor(along[:, :].rearrange("p (h d) -> p h d", h=NH), v_y,
                                       coef[:, :].unsqueeze(2).broadcast_to([P, NH, HD]), ALU.mult)\
                        .then_inc(s["along_ok"], 1)
                if live(x):
                    r = (k - 6) % 4
                    pool.indirect_dma_start(out=routed, out_offset=bass.IndirectOffsetOnAxis(ap=pos[:, r, :], axis=0),
                                            in_=rec[:, r, :], in_offset=None).then_inc(rec_out[r], 16)
                if live(i):
                    need(pool, s["val_ok"], i + 1)
                    need(pool, s["vvsum_raw"], i)
                    pool.tensor_tensor(vv[:, :], v_s[:, k % 4, :], v_s[:, k % 4, :], ALU.mult).then_inc(s["vv_ok"], 1)
                if live(n):
                    p = k % 2
                    need(pool, s["stats_ok"], n + 1)
                    pool.tensor_tensor(vareps[:, p], mv[:, p, 1:2], eps[:, :], ALU.add).then_inc(s["vareps_ok"], 1)
                    need(pool, s["vareps_ok"], n + 1)
                    need(pool, s["xn_ok"], n - 1)
                    pool.tensor_tensor(rstd[:, p], vareps[:, p], mhalf[:, :], ALU.pow).then_inc(s["rstd_ok"], 1)
            pool.wait_ge(s["consts_in"], 16 * 10)
            run_steps(pool, attention_step, -2, NT + 6)

            def expert_step(i, k):
                t, r = i + 1, (k + 1) % 4
                if live(i, NSLOT):
                    need(pool, s["g_y"], i + 1)
                    need(pool, s["g_token"], i + 1)
                if live(t, NSLOT):
                    need(pool, rec_in[r], arrivals(t, r, 4, 16))
                    if not isinstance(t, int) or t >= 4:
                        need(pool, y_out[r], arrivals(t - 4, r, 4, 16))
                    pool.tensor_tensor(token_of[:, r, :], slot_rec[:, r, R_TOK:R_TOK + 1].bitcast(U32), zero_u[:, :],
                                       ALU.add).then_inc(s["g_token"], 1)
                if not live(i, NSLOT):
                    return
                pool.indirect_dma_start(
                    out=out, out_offset=bass.IndirectOffsetOnAxis(ap=token_of[:, k, :], axis=0),
                    in_=yout[:, k, :], in_offset=None, bounds_check=NTOK - 1, oob_is_err=False).then_inc(y_out[k], 16)
            run_steps(pool, expert_step, -1, NSLOT, 8, 40)

        @block.vector
        def _(dve):
            dve.wait_ge(s["zeroed"], 5)
            for q in range(2):
                for b in range(2):
                    dve.memset(vd[0:S, q, b, :, HD:HD + 1], 1.0).then_inc(s["vd_ones"], 1)
                    dve.memset(vd[S:P, q, b, :, VW - 1:VW], 1.0).then_inc(s["vd_ones"], 1)
            def context_step(i, k):
                t, n, u = i + 1, i + 2, i - 1
                p, q = (k + 1) % 2, k % 2
                if live(n):
                    need(dve, x_in[(k + 2) % 4], arrivals(n, (k + 2) % 4, 4, 16))
                    need(dve, s["a_vareps"], n - 1)
                    dve.bn_stats(stats[:, q, :], rows(n)).then_inc(s["a_stats_raw"], 1)
                    need(dve, s["a_stats_raw"], n + 1)
                if live(t):
                    need(dve, s["a_rstd"], t + 1)
                    need(dve, s["a_xT_psum"], t - 1)
                    dve.tensor_scalar(xn[:, p, :], rows(t), mv[:, p, 0:1], rstd[:, p], ALU.subtract, ALU.mult)\
                        .then_inc(s["a_xn"], 1)
                if live(n):
                    dve.bn_aggr(mv[:, q, :], stats[:, q, :]).then_inc(s["a_stats"], 1)
                if live(u):
                    need(dve, s["norms_sbuf"], u + 1)
                    dve.reciprocal(rnorm[:, p, :], norm[:, p, :]).then_inc(s["norms_inv"], 1)
                    need(dve, s["norms_inv"], u + 1)
                    need(dve, s["dots_psum"], u + 1)
                    need(dve, s["tok_sum"], u - 1)
                    dve.scalar_tensor_tensor(cos[:, p, :], rnorm[:, p, :], 1.0 / COS_EPS, bank(6 + p, SC),
                                             ALU.min, ALU.mult).then_inc(s["cos_sbuf"], 1)
            run_steps(dve, context_step, -2, NT + 1)
            dve.wait_ge(s["consts_in"], 16 * 10)
            dve.wait_ge(s["consts_made"], 13)

            def attention_step(i, k):
                t, n, u, y, w, z = i + 1, i + 2, i - 1, i - 3, i - 4, i - 5
                r, zp, zr = (k - 4) % 4, (k - 5) % 2, (k - 5) % 4
                o_ps = bank(7, NH * (HD + 1)).rearrange("p (h d) -> p h d", h=NH)
                if live(w):
                    need(dve, s["wo_psum"], w + 1)
                    need(dve, s["bo_added"], w + 1)
                    if not isinstance(w, int) or w >= 4:
                        need(dve, rec_out[r], arrivals(w - 4, r, 4, 16))
                    dve.tensor_tensor(rec[:, r, 0:D], bank(6, D), rows(w), ALU.add).then_inc(s["x3_ok"], 1)
                if live(y):
                    need(dve, s["o_psum"], y + 1)
                    dve.reciprocal(rsum[:, :], o_ps[:, :, HD]).then_inc(s["rsum_ok"], 1)
                if live(w):
                    need(dve, s["x3_ok"], w + 1)
                    dve.bn_stats(stats3[:, :], rec[:, r, 0:D]).then_inc(s["stats3_raw"], 1)
                if live(z):
                    dve.max(top8[:, :], logit[:, zp, :]).then_inc(s["top_ok"], 1)
                if live(w):
                    need(dve, s["stats3_raw"], w + 1)
                if live(z):
                    need(dve, s["top_ok"], z + 1)
                    dve.tensor_scalar(ntop[:, zp, :], top8[:, 0:1], -1.0, None, ALU.mult).then_inc(s["ntop_ok"], 1)
                if live(w):
                    dve.bn_aggr(rec[:, r, R_MEAN:R_MEAN + 2], stats3[:, :]).then_inc(s["stats3_ok"], 1)
                if live(z):
                    dve.max_index(arg8[:, :], top8[:, :], logit[:, zp, :]).then_inc(s["arg_ok"], 1)
                if live(y):
                    need(dve, s["rsum_ok"], y + 1)
                    dve.tensor_tensor(o_n[:, :].rearrange("p (h d) -> p h d", h=NH), o_ps[:, :, 0:HD],
                                      rsum[:, :].unsqueeze(2).broadcast_to([P, NH, HD]), ALU.mult)\
                        .then_inc(s["on_ok"], 1)
                if live(z):
                    need(dve, s["arg_ok"], z + 1)
                    dve.tensor_copy(argf[:, zp, :], arg8[:, 0:1]).then_inc(s["argf_ok"], 1)
                if live(t):
                    p = (k + 1) % 2
                    need(dve, s["rstd_ok"], t + 1)
                    need(dve, s["xT_psum"], t - 1)
                    dve.tensor_scalar(xn[:, p, :], rows(t), mv[:, p, 0:1], rstd[:, p], ALU.subtract, ALU.mult)\
                        .then_inc(s["xn_ok"], 1)
                if live(z):
                    need(dve, s["argf_ok"], z + 1)
                    need(dve, s["rank_psum"], z - 1)
                    dve.tensor_scalar(onehot[:, zp, :], iota_e[:, :], argf[:, zp, :], None, ALU.is_equal)\
                        .then_inc(s["onehot_ok"], 1)
                if live(w):
                    need(dve, s["rstd3_ok"], w + 1)
                    need(dve, s["x3T_psum"], w - 1)
                    dve.tensor_scalar(x3n[:, k % 2, :], rec[:, r, 0:D], rec[:, r, R_MEAN:R_MEAN + 1],
                                      rec[:, r, R_RSTD:R_RSTD + 1], ALU.subtract, ALU.mult).then_inc(s["x3n_ok"], 1)
                if live(z):
                    need(dve, s["onehot_ok"], z + 1)
                    need(dve, s["rank_psum"], z)
                    dve.tensor_tensor(earlier[:, 1 - zp, :], earlier[:, zp, :], onehot[:, zp, :], ALU.add)\
                        .then_inc(s["earlier_ok"], 1)
                if live(i):
                    need(dve, s["val_psum"], i + 1)
                    need(dve, s["along_ok"], i - 3)
                    dve.tensor_tensor(v_s[:, k % 4, :], bank(6, D), bv_s[:, :], ALU.add).then_inc(s["val_ok"], 1)
                if live(y):
                    need(dve, s["ov_ok"], y + 1)
                    dve.tensor_reduce(dot[:, :], ov[:, :].rearrange("p (h d) -> p h d", h=NH), AX.X, ALU.add)\
                        .then_inc(s["dot_ok"], 1)
                    need(dve, s["dot_ok"], y + 1)
                    need(dve, s["rvv_ok"], y + 1)
                    dve.tensor_tensor(coef[:, :], dot[:, :], rvv[:, (k - 3) % 4, :], ALU.mult).then_inc(s["coef_ok"], 1)
                if live(n):
                    q = k % 2
                    need(dve, s["tok_sum"], n + 1)
                    need(dve, s["vareps_ok"], n - 1)
                    dve.bn_stats(stats[:, q, :], rows(n)).then_inc(s["stats_raw"], 1)
                    need(dve, s["stats_raw"], n + 1)
                if live(u):
                    need(dve, s["vv_ok"], u + 1)
                    dve.tensor_reduce(vvsum[:, :], vv[:, :].rearrange("p (h d) -> p h d", h=NH), AX.X, ALU.add)\
                        .then_inc(s["vvsum_raw"], 1)
                if live(n):
                    dve.bn_aggr(mv[:, q, :], stats[:, q, :]).then_inc(s["stats_ok"], 1)
                if live(y):
                    need(dve, s["along_ok"], y + 1)
                    need(dve, s["oT_psum"], y - 1)
                    dve.tensor_tensor(o_f[:, (k - 3) % 2, :], o_n[:, :], along[:, :], ALU.subtract).then_inc(s["of_ok"], 1)
                if live(z):
                    need(dve, s["rank_psum"], z + 1)
                    need(dve, s["l_psum"], w + 1, NT)
                    dve.tensor_tensor(ranked[:, :], bank(6)[:, 320:320 + E], onehot[:, zp, :], ALU.mult)\
                        .then_inc(s["ranked_ok"], 1)
                if live(w):
                    need(dve, s["l_psum"], w + 1)
                    need(dve, s["lsum_ok"], w - 1)
                    dve.tensor_copy(logit[:, k % 2, :], bank(6)[:, 352:352 + E]).then_inc(s["logit_ok"], 1)
                if live(z):
                    need(dve, s["ranked_ok"], z + 1)
                    dve.tensor_reduce(rank[:, :], ranked[:, :], AX.X, ALU.add).then_inc(s["rank_ok"], 1)
                if live(z):
                    need(dve, s["rank_ok"], z + 1)
                    dve.scalar_tensor_tensor(posf[:, :], argf[:, zp, :], float(REGION), rank[:, :], ALU.mult, ALU.add)\
                        .then_inc(s["posf_ok"], 1)
                if live(u):
                    need(dve, s["vvsum_raw"], u + 1)
                    dve.tensor_scalar(vvsum[:, :], vvsum[:, :], ATT_EPS, None, ALU.add).then_inc(s["rvv_raw"], 1)
                s_ps = psum[:, 0:NH * S].rearrange("p (h j) -> p h j", h=NH)
                if live(u):
                    need(dve, s["s_psum"], u + 1)
                    dve.tensor_reduce(smax[:, :], s_ps, AX.X, ALU.max).then_inc(s["smax_ok"], 1)
                if live(z):
                    need(dve, s["lsum_ok"], z + 1)
                    dve.reciprocal(rec[:, zr, R_PROB:R_PROB + 1], lsum[:, zp, :])
                    need(dve, s["posf_ok"], z + 1)
                    dve.tensor_copy(pos[:, zr, :], posf[:, :]).then_inc(s["pos_ok"], 1)
                if live(u):
                    need(dve, s["rvv_raw"], u + 1)
                    dve.reciprocal(rvv[:, (k - 1) % 4, :], vvsum[:, :]).then_inc(s["rvv_ok"], 1)
                if live(w):
                    need(dve, s["logit_ok"], w + 1)
                if live(u):
                    need(dve, s["smax_ok"], u + 1)
                    need(dve, s["pT_psum"], u - 1)
                    dve.tensor_tensor(prob[:, (k - 1) % 2, :].rearrange("p (h j) -> p h j", h=NH), s_ps,
                                      smax[:, :].unsqueeze(2).broadcast_to([P, NH, S]), ALU.subtract)\
                        .then_inc(s["centred"], 1)
            run_steps(dve, attention_step, -2, NT + 5)

            steps = [0]

            def then(instruction):
                steps[0] += 1
                instruction.then_inc(s["plan"], 1)
                dve.wait_ge(s["plan"], steps[0])
            dve.wait_ge(s["count_psum"], 1)
            dve.wait_ge(s["b2_in"], 16)
            then(dve.tensor_copy(counts[:, :], bank(7)[0:1, 384:384 + E]))
            then(dve.tensor_tensor(padf[:, :], counts[:, :], region0[:, :], ALU.add))
            then(dve.tensor_copy(pad_tab[:, :], padf[:, :]))
            then(dve.tensor_scalar(tiles_of[:, :], counts[:, :], float(P - 1), None, ALU.add))
            then(dve.tensor_copy(plan_i[:, :], tiles_of[:, :]))
            then(dve.tensor_scalar(plan_i[:, :], plan_i[:, :], 7, None, ALU.arith_shift_right))
            then(dve.tensor_copy(tiles_of[:, :], plan_i[:, :]))
            then(dve.tensor_copy(ends[:, 0, :], plan_i[:, :]))
            at, reach = 0, 1
            while reach < E:
                then(dve.tensor_copy(ends[:, 1 - at, 0:reach], ends[:, at, 0:reach]))
                then(dve.tensor_tensor(ends[:, 1 - at, reach:E], ends[:, at, reach:E], ends[:, at, 0:E - reach], ALU.add))
                at, reach = 1 - at, 2 * reach
            grid = [1, NSLOT, E]
            then(dve.tensor_tensor(passed[:, :, :], ends[:, at, :].unsqueeze(1).broadcast_to(grid), slot_no[:, :, :],
                                   ALU.is_le))
            then(dve.tensor_reduce(slot_e[:, :], passed[:, :, :], AX.X, ALU.add))
            then(dve.tensor_tensor(started[:, :, :], passed[:, :, :], tiles_of[:, :].unsqueeze(1).broadcast_to(grid),
                                   ALU.mult))
            then(dve.tensor_reduce(slot_s[:, :], started[:, :, :], AX.X, ALU.add))
            then(dve.tensor_tensor(slot_s[:, :], slot_no[:, :, 0], slot_s[:, :], ALU.subtract))
            then(dve.tensor_scalar(slot_s[:, :], slot_s[:, :], float(P), None, ALU.mult))
            then(dve.scalar_tensor_tensor(slot_b[:, :], slot_e[:, :], float(REGION), slot_s[:, :], ALU.mult, ALU.add))
            then(dve.tensor_scalar(slot_b[:, :], slot_b[:, :], float(E * REGION), None, ALU.min))
            then(dve.tensor_scalar(slot_e[:, :], slot_e[:, :], float(E - 1), None, ALU.min))
            then(dve.tensor_copy(expert_tab[:, :], slot_e[:, :]))
            dve.tensor_copy(base_tab[:, :], slot_b[:, :]).then_inc(s["plan_ok"], 1)

            def expert_step(i, k):
                t, u = i + 1, i - 1
                if live(t, NSLOT):
                    r = (k + 1) % 4
                    need(dve, rec_in[r], arrivals(t, r, 4, 16))
                    need(dve, s["g_xT_psum"], t - 1)
                    dve.tensor_scalar(xg[:, r % 2, :], slot_rec[:, r, 0:D], slot_rec[:, r, R_MEAN:R_MEAN + 1],
                                      slot_rec[:, r, R_RSTD:R_RSTD + 1], ALU.subtract, ALU.mult).then_inc(s["g_xg"], 1)
                if live(i, NSLOT):
                    need(dve, s["g_h_psum"], i + 1)
                    need(dve, s["g_hT_psum"], i - 1)
                    dve.tensor_copy(hid[:, k % 2, :], bank(k % 2)).then_inc(s["g_h"], 1)
                if live(u, NSLOT):
                    r = (k - 1) % 4
                    p = r % 2
                    e = dve.value_load(expert_tab[0:1, bass.ds(u, 1)], min_val=0, max_val=E - 1)
                    need(dve, s["g_y_psum"], u + 1)
                    dve.tensor_tensor(ysum[:, p, :], bank(2 + p, D), b2_s[:, bass.ds(e * D, D)], ALU.add)\
                        .then_inc(s["g_ysum"], 1)
                    need(dve, s["g_ysum"], u + 1)
                    if not isinstance(u, int) or u >= 4:
                        need(dve, y_out[r], arrivals(u - 4, r, 4, 16))
                    dve.scalar_tensor_tensor(yout[:, r, :], ysum[:, p, :], slot_rec[:, r, R_PROB:R_PROB + 1],
                                             slot_rec[:, r, 0:D], ALU.mult, ALU.add).then_inc(s["g_y"], 1)
            run_steps(dve, expert_step, -1, NSLOT + 1, 8, 40)

        @block.scalar
        def _(act):
            act.preload_act_table(ACT.Sqrt)
            act.wait_ge(s["a_consts_in"], 64)

            def context_step(i, k):
                t, p, u, q = i, k % 2, i - 1, (k - 1) % 2
                if live(t):
                    need(act, s["a_xT_psum"], t + 1)
                    need(act, s["v_psum"], t - 1)
                    act.activation(xnT[:, p, :], bank(0, D), ACT.Copy).then_inc(s["a_xT"], 1)
                    need(act, s["t_psum"], t + 1)
                    need(act, s["dots_psum"], t - 1)
                    act.activation(tT[:, p, :], bank(2 + p), ACT.Identity, bias=xbt_s[:, 0:1])
                    need(act, s["v_psum"], t + 1)
                    act.activation(vsq[:, p, :], bank(1, P), ACT.Square, bias=xbv_s[:, 0:1])
                    act.activation(vT[:, p, :], bank(1, P), ACT.Identity, bias=xbv_s[:, 0:1]).then_inc(s["v_sbuf"], 1)
                    act.activation(tsq[:, p, :], bank(2 + p), ACT.Square, bias=xbt_s[:, 0:1]).then_inc(s["t_sbuf"], 1)
                if live(u):
                    need(act, s["norms_psum"], u + 1)
                    need(act, s["norms_inv"], u - 1)
                    act.activation(norm[:, q, :], bank(4 + q, SC), ACT.Sqrt).then_inc(s["norms_sbuf"], 1)
                if live(t):
                    need(act, s["vnorm_psum"], t + 1)
                    act.activation(vnorm[:, p, :], bank(1)[:, P:2 * P], ACT.Copy).then_inc(s["vnorm_sbuf"], 1)
            run_steps(act, context_step, 0, NT + 1)
            act.preload_act_table(ACT.Exp)
            act.wait_ge(s["consts_in"], 16 * 10)
            act.wait_ge(s["zeroed"], 5)
            act.wait_ge(s["vd_ones"], 8)

            def attention_step(i, k):
                p, t, u, v, y, w, z = k % 2, i + 1, i - 1, i - 2, i - 3, i - 4, i - 5
                if live(z):
                    zp = (k - 5) % 2
                    need(act, s["ntop_ok"], z + 1)
                    need(act, s["pos_ok"], z - 1)
                    act.activation(expl[:, :], logit[:, zp, :], ACT.Exp, bias=ntop[:, zp, :], accum_out=lsum[:, zp, :])\
                        .then_inc(s["lsum_ok"], 1)
                if live(i):
                    need(act, s["qk_psum"], i + 1)
                    if not isinstance(i, int) or i >= 2:
                        need(act, kd_in[p], arrivals(i - 2, p, 2, 128))
                    for c in range(KC):
                        last = act.activation(kT[:, p, c * P:(c + 1) * P], bank(4)[:, c * P:(c + 1) * P],
                                              ACT.Identity, bias=bk_s[:, c:c + 1])
                    last.then_inc(s["k_ok"], 1)
                if live(w):
                    need(act, s["x3T_psum"], w + 1)
                    need(act, s["l_psum"], w - 1)
                    act.activation(x3T[:, p, :], bank(5, D), ACT.Copy).then_inc(s["x3T_ok"], 1)
                if live(v):
                    need(act, s["pT_psum"], v + 1)
                    need(act, s["o_psum"], v - 1)
                    act.activation(probT[:, p, :], psum[:, 1024:2048], ACT.Copy).then_inc(s["pT_ok"], 1)
                if live(i):
                    need(act, s["s_psum"], i - 1)
                    for c in range(KC):
                        last = act.activation(qT[:, p, c * P:(c + 1) * P], bank(4)[:, (KC + c) * P:(KC + c + 1) * P],
                                              ACT.Identity, bias=bq_s[:, c:c + 1])
                    last.then_inc(s["q_ok"], 1)
                if live(u):
                    q, r = (k - 1) % 2, (k - 1) % 4
                    need(act, swap_in[q], arrivals(u, q, 2, 32))
                    need(act, s["o_psum"], u - 1)

                    def heads(tile, odd):
                        return tile.rearrange("p (n o d) -> p n o d", n=NPAIR, o=2)[:, :, odd]
                    act.activation(vd[0:S, q, 0, :, 0:HD], heads(v_s[0:S, r, :], 0), ACT.Copy)
                    act.activation(vd[S:P, q, 0, :, HD + 1:VW - 1], heads(v_swap[S:P, q, :], 1), ACT.Copy)
                    act.activation(vd[0:S, q, 1, :, 0:HD], heads(v_swap[0:S, q, :], 0), ACT.Copy)
                    act.activation(vd[S:P, q, 1, :, HD + 1:VW - 1], heads(v_s[S:P, r, :], 1), ACT.Copy)\
                        .then_inc(s["vd_ok"], 1)
                if live(y):
                    q = (k - 3) % 2
                    need(act, s["oT_psum"], y + 1)
                    need(act, s["wo_psum"], y - 1)
                    act.activation(oT[:, q, :], bank(5, D), ACT.Copy).then_inc(s["oT_ok"], 1)
                if live(t):
                    need(act, s["xT_psum"], t + 1)
                    need(act, s["val_psum"], t - 1)
                    act.activation(xnT[:, 1 - p, :], bank(5, D), ACT.Copy).then_inc(s["xT_ok"], 1)
                if live(u):
                    q = (k - 1) % 2
                    need(act, s["centred"], u + 1)
                    act.activation(prob[:, q, :], prob[:, q, :], ACT.Exp, scale=HD ** -0.5).then_inc(s["exp_ok"], 1)
            run_steps(act, attention_step, -1, NT + 5)
            act.preload_act_table(ACT.Gelu)
            act.wait_ge(s["plan_ok"], 1)

            def expert_step(i, k):
                t = i + 1
                if live(t, NSLOT):
                    q = (k + 1) % 2
                    need(act, s["g_xT_psum"], t + 1)
                    need(act, s["g_h_psum"], t - 1)
                    act.activation(xgT[:, q, :], bank(6 + q, D), ACT.Copy).then_inc(s["g_xT"], 1)
                if live(i, NSLOT):
                    p = k % 2
                    e = act.value_load(expert_tab[0:1, bass.ds(i, 1)], min_val=0, max_val=E - 1)
                    need(act, s["g_hT_psum"], i + 1)
                    need(act, s["g_y_psum"], i - 1)
                    for f in range(FC):
                        last = act.activation(hidT[:, p, f * P:(f + 1) * P], bank(4 + p)[:, f * P:(f + 1) * P], ACT.Gelu,
                                              bias=b1_s[:, bass.ds(e * FC + f, 1)])
                    last.then_inc(s["g_hT"], 1)
            run_steps(act, expert_step, -1, NSLOT, 8, 40)

        @block.tensor
        def _(pe):
            pe.wait_ge(s["a_consts_in"], 64)
            pe.wait_ge(s["consts_made"], 13)

            def turn(tile, source, signal):
                for c in range(KC):
                    mm = pe.transpose(tile[:, c * P:(c + 1) * P], source[:, c * P:(c + 1) * P], ident[:, :])
                mm.then_inc(signal, 1)

            def context_step(i, k):
                t, p, u, q = i, k % 2, i - 1, (k - 1) % 2
                if live(t):
                    need(pe, s["a_xn"], t + 1)
                    need(pe, s["a_xT"], t)
                    turn(bank(0), xn[:, p, :], s["a_xT_psum"])
                    need(pe, ctx_in[k], arrivals(t, k, 4, 16))
                    need(pe, s["t_sbuf"], t - 1)
                    for c in range(2):
                        mm = pe.matmul(bank(2 + p), wt_s[:, c, :], ctx_in_sb[0:CK, k, c, :], start=c == 0, stop=c == 1)
                    mm.then_inc(s["t_psum"], 1)
                    need(pe, s["a_xT"], t + 1)
                    need(pe, s["vnorm_sbuf"], t)
                    for c in range(KC):
                        mm = pe.matmul(bank(1, P), wv_s[:, c, :], xnT[:, p, c * P:(c + 1) * P], start=c == 0,
                                       stop=c == KC - 1)
                    mm.then_inc(s["v_psum"], 1)
                if live(u):
                    need(pe, s["t_sbuf"], u + 1)
                    need(pe, s["vnorm_sbuf"], u + 1)
                    need(pe, s["norms_sbuf"], u - 1)
                    for b in range(2):
                        h = slice(b * S, (b + 1) * S)
                        mm = pe.matmul(bank(4 + q, SC)[h, :], vnorm[:, q, h], tsq[:, q, b * SC:(b + 1) * SC],
                                       start=True, stop=True)
                    mm.then_inc(s["norms_psum"], 1)
                    need(pe, s["cos_sbuf"], u - 1)
                    for b in range(2):
                        h = slice(b * S, (b + 1) * S)
                        mm = pe.matmul(bank(6 + q, SC)[h, :], vT[:, q, h], tT[:, q, b * SC:(b + 1) * SC],
                                       start=True, stop=True)
                    mm.then_inc(s["dots_psum"], 1)
                if live(t):
                    need(pe, s["v_sbuf"], t + 1)
                    pe.matmul(bank(1)[:, P:2 * P], ones[:, :], vsq[:, p, :], start=True, stop=True)\
                        .then_inc(s["vnorm_psum"], 1)
            run_steps(pe, context_step, 0, NT + 1)
            pe.wait_ge(s["consts_in"], 16 * 10)
            pe.wait_ge(s["cos_sbuf"], NT)

            def attention_step(i, k):
                p, t, u, v, y, w, z = k % 2, i + 1, i - 1, i - 2, i - 3, i - 4, i - 5

                def scores(c):
                    q = (k - 1) % 2
                    for b in range(2):
                        h = slice(b * S, (b + 1) * S)
                        mm = pe.matmul(bank(c)[h, :], qT[:, q, c * P + b * S:c * P + (b + 1) * S], kd[:, q, c, b, :],
                                       start=True, stop=True)
                    return mm
                if live(i):
                    need(pe, s["xT_ok"], i + 1)
                    need(pe, s["q_ok"], i)
                    for m, weight in enumerate((wk_s, wq_s)):
                        for c in range(KC):
                            at = (m * KC + c) * P
                            for d in range(KC):
                                mm = pe.matmul(bank(4)[:, at:at + P], weight[:, d, c * P:(c + 1) * P],
                                               xnT[:, p, d * P:(d + 1) * P], start=d == 0, stop=d == KC - 1)
                    mm.then_inc(s["qk_psum"], 1)
                if live(v):
                    need(pe, s["exp_ok"], v + 1)
                    need(pe, s["pT_ok"], v)
                    for n in range(NPAIR):
                        mm = pe.transpose(psum[:, 1024 + n * P:1024 + (n + 1) * P], prob[:, p, n * P:(n + 1) * P],
                                          ident[:, :])
                    mm.then_inc(s["pT_psum"], 1)
                if live(i):
                    need(pe, s["val_ok"], i)
                    need(pe, s["x3_ok"], i - 3)
                    for d in range(KC):
                        mm = pe.matmul(bank(6, D), xnT[:, p, d * P:(d + 1) * P], av_s[:, d, :], start=d == 0,
                                       stop=d == KC - 1)
                    mm.then_inc(s["val_psum"], 1)
                if live(w):
                    need(pe, s["x3n_ok"], w + 1)
                    need(pe, s["oT_ok"], w + 1)
                    need(pe, s["xT_ok"], i + 1, NT)
                    turn(bank(5), x3n[:, p, :], s["x3T_psum"])
                if live(u):
                    q = (k - 1) % 2
                    need(pe, kd_in[q], arrivals(u, q, 2, 128))
                    need(pe, s["q_ok"], u + 1)
                    need(pe, s["centred"], u)
                    scores(0)
                if live(z):
                    zp = (k - 5) % 2
                    need(pe, s["val_ok"], i + 1, NT)
                    need(pe, s["earlier_ok"], z)
                    need(pe, s["onehot_ok"], z + 1)
                    pe.matmul(bank(6)[:, 320:320 + E], before16[:, :], onehot[:, zp, :], start=True, stop=False)
                    pe.matmul(bank(6)[:, 320:320 + E], ones16[:, :], earlier[:, zp, :], start=False, stop=True)\
                        .then_inc(s["rank_psum"], 1)
                if live(w):
                    need(pe, s["x3T_ok"], w + 1)
                    need(pe, s["val_ok"], i + 1, NT)
                    for d in range(KC):
                        mm = pe.matmul(bank(6)[:, 352:352 + E], x3T[:, p, d * P:(d + 1) * P], rt_s[:, d, :],
                                       start=d == 0, stop=d == KC - 1)
                    mm.then_inc(s["l_psum"], 1)
                if live(u):
                    scores(1).then_inc(s["s_psum"], 1)
                if live(y):
                    q = (k - 3) % 2
                    need(pe, s["of_ok"], y + 1)
                    need(pe, s["x3T_ok"], w + 1, NT)
                    turn(bank(5), o_f[:, q, :], s["oT_psum"])
                if live(v):
                    need(pe, s["pT_ok"], v + 1)
                    need(pe, s["vd_ok"], v + 1)
                    need(pe, s["on_ok"], v)
                    for n in range(NPAIR):
                        for b in range(2):
                            h = slice(b * S, (b + 1) * S)
                            mm = pe.matmul(bank(7)[h, n * VW:(n + 1) * VW], probT[:, p, n * P + b * S:n * P + (b + 1) * S],
                                           vd[:, p, b, n, :], start=True, stop=True)
                    mm.then_inc(s["o_psum"], 1)
                if live(t):
                    need(pe, s["xn_ok"], t + 1)
                    need(pe, s["x3T_ok"], w + 1)
                    need(pe, s["oT_ok"], y + 1)
                    turn(bank(5), xn[:, 1 - p, :], s["xT_psum"])
                if live(y):
                    need(pe, s["x3_ok"], y)
                    need(pe, s["val_ok"], i + 1, NT)
                    need(pe, s["oT_ok"], y + 1)
                    need(pe, s["logit_ok"], w + 1, NT)
                    need(pe, s["ranked_ok"], z + 1, NT)
                    for d in range(KC):
                        mm = pe.matmul(bank(6, D), oT[:, q, d * P:(d + 1) * P], wo_s[:, d, :], start=d == 0,
                                       stop=d == KC - 1)
                    mm.then_inc(s["wo_psum"], 1)
            run_steps(pe, attention_step, -1, NT + 5)
            pe.wait_ge(s["earlier_ok"], NT)
            pe.wait_ge(s["ranked_ok"], NT)
            pe.matmul(bank(7)[:, 384:384 + E], ones16[:, :], earlier[:, NT % 2, :], start=True, stop=True)\
                .then_inc(s["count_psum"], 1)
            pe.wait_ge(s["plan_ok"], 1)
            pe.wait_ge(s["weights_in"], 16 * (HI - LO + 4))

            def expert_step(i, k):
                t, p, u, q = i + 1, k % 2, i - 1, (k - 1) % 2
                if live(i, NSLOT):
                    e = pe.value_load(expert_tab[0:1, bass.ds(i, 1)], min_val=0, max_val=E - 1)
                    need(pe, s["g_xT"], i + 1)
                    need(pe, s["g_h"], i - 1)
                    for c in range(KC):
                        mm = pe.matmul(bank(p), xgT[:, p, c * P:(c + 1) * P], W[:, bass.ds(e * EW + c * F, F)],
                                       start=c == 0, stop=c == KC - 1)
                    mm.then_inc(s["g_h_psum"], 1)
                if live(u, NSLOT):
                    e = pe.value_load(expert_tab[0:1, bass.ds(u, 1)], min_val=0, max_val=E - 1)
                if live(t, NSLOT):
                    need(pe, s["g_xg"], t + 1)
                    need(pe, s["g_xT"], t - 1)
                    turn(bank(6 + (k + 1) % 2), xg[:, (k + 1) % 2, :], s["g_xT_psum"])
                if live(u, NSLOT):
                    need(pe, s["g_hT"], u + 1)
                    need(pe, s["g_ysum"], u - 1)
                    for f in range(FC):
                        mm = pe.matmul(bank(2 + q, D), hidT[:, q, f * P:(f + 1) * P],
                                       W[:, bass.ds(e * EW + KC * F + f * D, D)], start=f == 0, stop=f == FC - 1)
                    mm.then_inc(s["g_y_psum"], 1)
                if live(i, NSLOT):
                    need(pe, s["g_h"], i + 1)
                    need(pe, s["g_hT"], i - 1)
                    for f in range(FC):
                        mm = pe.transpose(bank(4 + p)[:, f * P:(f + 1) * P], hid[:, p, f * P:(f + 1) * P], ident[:, :])
                    mm.then_inc(s["g_hT_psum"], 1)
            run_steps(pe, expert_step, -1, NSLOT + 1, 8, 40)


def rows_first(a, parts):
    n = a.shape[0] // parts
    return np.ascontiguousarray(a.reshape(parts, n, a.shape[1]).transpose(1, 0, 2))


def columns(a):
    return np.ascontiguousarray(a.reshape(-1, P).T)


def lay_out(x, ctx_768, L0_xattn_Wv, L0_xattn_bv, L0_xattn_Wt, L0_xattn_bt, L0_attn_wq, L0_attn_bq, L0_attn_wk,
            L0_attn_bk, L0_attn_wv, L0_attn_bv, L0_attn_wo, L0_attn_bo, L0_ffn_router_w, L0_ffn_w1, L0_ffn_b1,
            L0_ffn_w2, L0_ffn_b2):
    w1 = L0_ffn_w1.reshape(E, KC, P, F).transpose(0, 2, 1, 3).reshape(E, P, KC * F)
    w2 = L0_ffn_w2.reshape(E, FC, P, D).transpose(0, 2, 1, 3).reshape(E, P, FC * D)
    return {
        "x": np.ascontiguousarray(x.reshape(NTOK, D)),
        "ctxT": np.ascontiguousarray(ctx_768.reshape(NT, 2 * SC, 2, CK).transpose(0, 3, 2, 1)),
        "wvT": rows_first(L0_xattn_Wv.T, KC),
        "wtT": rows_first(L0_xattn_Wt.T, 2),
        "xbv": columns(L0_xattn_bv),
        "xbt": columns(L0_xattn_bt),
        "wqT": rows_first(L0_attn_wq.T, KC),
        "wkT": rows_first(L0_attn_wk.T, KC),
        "avT": rows_first(L0_attn_wv.T, KC),
        "woT": rows_first(L0_attn_wo.T, KC),
        "bq": columns(L0_attn_bq),
        "bk": columns(L0_attn_bk),
        "bv": np.ascontiguousarray(L0_attn_bv.reshape(1, D)),
        "bo": np.ascontiguousarray(L0_attn_bo.reshape(1, D)),
        "routerT": rows_first(L0_ffn_router_w, KC),
        "weights": np.ascontiguousarray(np.stack([w1, w2], axis=1).reshape(2 * E, P, EW // 2)),
        "b1T": np.ascontiguousarray(L0_ffn_b1.reshape(E * FC, P).T),
        "b2": np.ascontiguousarray(L0_ffn_b2.reshape(1, E * D)),
    }


def kernel(**inputs):
    import concourse.bacc as bacc
    from concourse.bass_utils import run_bass_kernel_spmd

    nc = bacc.Bacc("TRN2", target_bir_lowering=False, num_devices=1)
    arrays = lay_out(**{n: np.asarray(a) for n, a in inputs.items()})
    args = {n: nc.dram_tensor(n, a.shape, F32, kind="ExternalInput").ap() for n, a in arrays.items()}
    args["out"] = nc.dram_tensor("out", (NTOK, D), F32, kind="ExternalOutput").ap()
    build(nc, **args)
    result = run_bass_kernel_spmd(nc, [arrays], core_ids=[0])
    return result.results[0]["out"].reshape(B, S, D)
```

```python
from contextlib import ExitStack

import numpy as np

import concourse.bass as bass
from concourse import mybir

F32 = mybir.dt.float32
BF16 = mybir.dt.bfloat16
U32 = mybir.dt.uint32
I32 = mybir.dt.int32
ALU = mybir.AluOpType
ACT = mybir.ActivationFunctionType
AX = mybir.AxisListType

P = 128
B, S, D = 64, 64, 256
SC, DC, H = 256, 192, 128
NH, HD = 16, 16
E, F = 14, 512
NTOK = B * S
NT = NTOK // P
CK = DC // 2
KC = D // P
FC = F // P
HC = P // HD
NPAIR = NH // 2
VW = 2 * (HD + 1)
EW = KC * F + FC * D
NSLOT = NTOK // P + E - 1
EVEN = -(-(NTOK // P + E // 2) // 4) * 4
REGION = NTOK + P
PAD0 = 8
REC = 264
R_RSTD, R_MEAN, R_VAR, R_PROB, R_TOK = D, D + 1, D + 2, D + 3, D + 4
NOWHERE = 1 << 20
LN_EPS, ATT_EPS, COS_EPS = 1e-5, 1e-8, 1e-8
ZEROED, CONSTS = 8, 11
LO, HI = 8, 28
TURN = 4


def need(engine, semaphore, value, most=None):
    if isinstance(value, int):
        if value <= 0:
            return
        if most is not None:
            value = min(value, most)
    engine.wait_ge(semaphore, value)


def run_steps(engine, step, first, last, lo=LO, hi=HI, turn=TURN):
    for i in range(first, lo):
        step(i, i % turn)
    with engine.Fori(0, (hi - lo) // turn) as n:
        for k in range(turn):
            step(n * turn + (lo + k), (lo + k) % turn)
    for i in range(hi, last):
        step(i, i % turn)


def live(t):
    return not isinstance(t, int) or 0 <= t < NT


def run_slots(engine, step, first, last, used_tab):
    run_steps(engine, lambda i, k: step(i, k, (0, EVEN)), first, EVEN + last, LO, EVEN - 4)
    used = engine.value_load(used_tab[0:1, 0:1], min_val=0, max_val=NSLOT)
    with engine.If(used > EVEN):
        for i in range(EVEN + first, NSLOT + last):
            step(i, i % 4, (EVEN, NSLOT))


def within(t, part):
    return not isinstance(t, int) or part[0] <= t < part[1]


def arrivals(t, slot, ring, each):
    if isinstance(t, int):
        return each * (t // ring + 1)
    return (t - slot) * (each // ring) + each


def build(nc, x, ctxT, wvT, wtT, xbv, xbt, wqT, wkT, avT, woT, bq, bk, bv, bo, routerT, weights, b1T, b2, out):
    routed = nc.dram_tensor("routed", ((E + 1) * REGION, REC), F32).ap()
    ctx = ExitStack()
    with ctx:
        def sb(name, shape, dtype=F32):
            return ctx.enter_context(nc.sbuf_tensor(name, shape, dtype))

        def sem(name):
            return ctx.enter_context(nc.semaphore(name))

        W = sb("W", [P, E * EW])
        ctx_in_sb = W[:, 0:2 * EW].rearrange("p (s c j) -> p s c j", s=4, c=2)
        tT = W[:, 2 * EW:2 * EW + 2 * F].rearrange("p (s j) -> p s j", s=2)
        tsq = W[:, 2 * EW + 2 * F:3 * EW].rearrange("p (s j) -> p s j", s=2)
        early = W[:, 3 * EW:3 * EW + 18 * P]
        vT, vsq, vnorm = (early[:, n * D:(n + 1) * D].rearrange("p (s j) -> p s j", s=2) for n in range(3))
        norm, rnorm, cos = (early[:, 6 * P + n * 2 * SC:6 * P + (n + 1) * 2 * SC].rearrange("p (s j) -> p s j", s=2)
                            for n in range(3))
        tok = W[:, (E - 4) * EW:E * EW]

        def rows(t):
            return tok[:, bass.ds(t * D, D)]

        wv_s = sb("wv_s", [P, KC, H])
        wt_s = sb("wt_s", [CK, 2, H])
        wq_s = sb("wq_s", [P, KC, D])
        wk_s = sb("wk_s", [P, KC, D])
        av_s = sb("av_s", [P, KC, D])
        wo_s = sb("wo_s", [P, KC, D])
        rt_s = sb("rt_s", [P, KC, E])
        xbv_s = sb("xbv_s", [P, 1])
        xbt_s = sb("xbt_s", [P, 1])
        bq_s = sb("bq_s", [P, KC])
        bk_s = sb("bk_s", [P, KC])
        bv_s = sb("bv_s", [P, D])
        bo_s = sb("bo_s", [P, D])
        b1_s = sb("b1_s", [P, E * FC])
        ident = sb("ident", [P, P])
        ones = sb("ones", [P, P])
        ones16 = sb("ones16", [P, P], BF16)
        before16 = sb("before16", [P, P], BF16)
        mhalf = sb("mhalf", [P, 1])
        eps = sb("eps", [P, 1])
        zero_u = sb("zero_u", [P, 1], U32)
        token_of = sb("token_of", [P, 4, 1], U32)
        iota_e = sb("iota_e", [P, E])
        token_ids = sb("token_ids", [P, NT], U32)
        slot_no = sb("slot_no", [P, 1])
        slot_off = sb("slot_off", [P, 1])
        region0 = sb("region0", [P, E])
        pad_rec = sb("pad_rec", [P, REC])

        arena = sb("arena", [P, 10560])
        kd = arena[:, 0:4096].rearrange("p (s c b j) -> p s c b j", s=2, c=KC, b=2)
        prob = arena[:, 4096:6144].rearrange("p (s j) -> p s j", s=2)
        probT = arena[:, 6144:8192].rearrange("p (s j) -> p s j", s=2)
        vd = arena[:, 8192:8192 + 4 * NPAIR * VW].rearrange("p (s b n j) -> p s b n j", s=2, b=2, n=NPAIR)
        hid = arena[:, 0:1024].rearrange("p (s j) -> p s j", s=2)
        hidT = arena[:, 1024:2048].rearrange("p (s j) -> p s j", s=2)
        xg = arena[:, 2048:2560].rearrange("p (s j) -> p s j", s=2)
        xgT = arena[:, 2560:3072].rearrange("p (s j) -> p s j", s=2)
        ysum = arena[:, 3072:3584].rearrange("p (s j) -> p s j", s=2)
        yout = arena[:, 3584:4608].rearrange("p (s j) -> p s j", s=4)
        slot_rec = arena[:, 4608:4608 + 4 * REC].rearrange("p (s j) -> p s j", s=4)
        b2_s = arena[:, 5664:5664 + E * D]

        xn = sb("xn", [P, 2, D])
        xnT = sb("xnT", [P, 2, D])
        stats = sb("stats", [P, 2, 6])
        mv = sb("mv", [P, 2, 2])
        vareps = sb("vareps", [P, 2, 1])
        rstd = sb("rstd", [P, 2, 1])

        qT = sb("qT", [P, 2, KC * P])
        kT = sb("kT", [P, 2, KC * P])
        v_s = sb("v_s", [P, 4, D])
        v_swap = sb("v_swap", [P, 2, D])
        vv = sb("vv", [P, D])
        vvsum = sb("vvsum", [P, NH])
        rvv = sb("rvv", [P, 4, NH])
        smax = sb("smax", [P, NH])
        rsum = sb("rsum", [P, NH])
        o_n = sb("o_n", [P, D])
        ov = sb("ov", [P, D])
        dot = sb("dot", [P, NH])
        coef = sb("coef", [P, NH])
        along = sb("along", [P, D])
        o_f = sb("o_f", [P, 2, D])
        oT = sb("oT", [P, 2, D])
        stats3 = sb("stats3", [P, 6])
        vareps3 = sb("vareps3", [P, 1])
        x3n = sb("x3n", [P, 2, D])
        x3T = sb("x3T", [P, 2, D])
        rec = sb("rec", [P, 4, REC])
        logit = sb("logit", [P, 2, E])
        top8 = sb("top8", [P, 8])
        arg8 = sb("arg8", [P, 8], U32)
        argf = sb("argf", [P, 2, 1])
        ntop = sb("ntop", [P, 2, 1])
        onehot = sb("onehot", [P, 2, E], BF16)
        earlier = sb("earlier", [P, 2, E], BF16)
        expl = sb("expl", [P, E])
        lsum = sb("lsum", [P, 2, 1])
        ranked = sb("ranked", [P, E])
        rank = sb("rank", [P, 1])
        posf = sb("posf", [P, 1])
        pos = sb("pos", [P, 4, 1], U32)
        counts = sb("counts", [NSLOT, E])
        plan_i = sb("plan_i", [NSLOT, E], I32)
        ends = sb("ends", [NSLOT, 2, PAD0 + E])
        origin = sb("origin", [NSLOT, E + 1])
        rise = sb("rise", [NSLOT, E])
        passed = sb("passed", [NSLOT, E])
        risen = sb("risen", [NSLOT, E])
        slot_e = sb("slot_e", [NSLOT, 1])
        slot_b = sb("slot_b", [NSLOT, 1])
        expert_tab = sb("expert_tab", [1, NSLOT], I32)
        base_tab = sb("base_tab", [1, NSLOT], I32)
        used_tab = sb("used_tab", [1, 1], I32)

        psum = ctx.enter_context(nc.psum_tensor("psum", [P, 8 * 512], F32))

        def bank(n, width=512):
            return psum[:, n * 512:n * 512 + width]

        x_in = [sem(f"x_in{n}") for n in range(4)]
        ctx_in = [sem(f"ctx_in{n}") for n in range(4)]
        kd_in = [sem(f"kd_in{n}") for n in range(2)]
        swap_in = [sem(f"swap_in{n}") for n in range(2)]
        rec_out = [sem(f"rec_out{n}") for n in range(4)]
        rec_in = [sem(f"rec_in{n}") for n in range(4)]
        y_out = [sem(f"y_out{n}") for n in range(4)]
        names = """
            first_made
            a_consts_in consts_in zeroed consts_made vd_ones weights_in b2_in pads_out
            a_stats_raw a_stats a_vareps a_rstd a_xn a_xT_psum a_xT t_psum t_sbuf v_psum v_sbuf
            vnorm_psum vnorm_sbuf norms_psum dots_psum norms_sbuf norms_inv cos_sbuf tok_sum
            stats_raw stats_ok vareps_ok rstd_ok xn_ok xT_psum xT_ok qk_psum k_ok q_ok
            val_psum val_ok vv_ok vvsum_raw rvv_raw rvv_ok vd_ok kd_ok s_psum smax_ok centred exp_ok pT_psum pT_ok
            o_psum rsum_ok on_ok ov_ok dot_ok coef_ok along_ok of_ok oT_psum oT_ok wo_psum x3_ok
            bo_added stats3_raw stats3_ok vareps3_ok rstd3_ok x3n_ok x3T_psum x3T_ok l_psum logit_ok
            top_ok arg_ok argf_ok ntop_ok onehot_ok earlier_ok lsum_ok token_ok rank_psum ranked_ok rank_ok
            posf_ok pos_ok count_psum plan columns_ok rows_psum plan_ok
            g_token g_xg g_xT_psum g_xT g_h_psum g_h g_hT_psum g_hT g_y_psum g_ysum g_y
        """.split()
        s = {n: sem(n) for n in names}

        block = ctx.enter_context(nc.Block())

        @block.sync
        def _(sp):
            rest = [(wq_s[:, :, :], wqT), (wk_s[:, :, :], wkT), (av_s[:, :, :], avT), (wo_s[:, :, :], woT),
                    (rt_s[:, :, :], routerT), (bq_s[:, :], bq), (bk_s[:, :], bk), (b1_s[:, :], b1T),
                    (bv_s[:, :], bv.broadcast_to([P, D])), (bo_s[:, :], bo.broadcast_to([P, D]))]

            def load_tokens(i, k):
                if isinstance(i, int) and i == 4:
                    for to, source in rest:
                        sp.dma_start(to, source).then_inc(s["consts_in"], 16)
                need(sp, x_in[k], arrivals(i - 4, k, 4, 16))
                sp.dma_start(rows(i), x[bass.ds(i * P, P), :]).then_inc(x_in[k], 16)
                need(sp, s["t_psum"], i - 3)
                sp.dma_start(ctx_in_sb[0:CK, k], ctxT[bass.ds(i, 1)].rearrange("o p c j -> (o p) c j"))\
                    .then_inc(ctx_in[k], 16)
            run_steps(sp, load_tokens, 0, NT)

            sp.wait_ge(s["consts_made"], CONSTS)
            sp.dma_start(routed.rearrange("(e r) c -> r e c", r=REGION)[0:P],
                         pad_rec[:, :].unsqueeze(1).broadcast_to([P, E + 1, REC])).then_inc(s["pads_out"], 16)
            sp.wait_ge(s["zeroed"], ZEROED)
            sp.wait_ge(s["cos_sbuf"], NT)

            def load_expert(e):
                sp.dma_start(W[:, e * EW:(e + 1) * EW].rearrange("p (h j) -> p h j", h=2),
                             weights[2 * e:2 * e + 2].rearrange("h p j -> p h j")).then_inc(s["weights_in"], 16)

            def attention_moves(i, k):
                p = k % 2
                if live(i):
                    need(sp, s["s_psum"], i - 1)
                if not isinstance(i, int):
                    half = i - LO
                    sp.dma_start(W[:, bass.ds(half * (EW // 2), EW // 2)],
                                 weights[bass.ds(half, 1)].rearrange("o p j -> (o p) j")).then_inc(s["weights_in"], 16)
                elif i == HI:
                    sp.wait_ge(s["x3_ok"], 16)
                    load_expert(E - 4)
                    load_expert(E - 3)
                elif i == HI + 2:
                    sp.wait_ge(s["x3_ok"], 24)
                    load_expert(E - 2)
                if live(i):
                    need(sp, s["k_ok"], i + 1)
                    for h in range(1, HC, 2):
                        r = slice(h * HD, (h + 1) * HD)
                        sp.dma_start(kd[r, p, :, :, h * S:(h + 1) * S].rearrange("p c b j -> p (c b) j"),
                                     kT[r, p, :].rearrange("p (n j) -> p n j", j=S)).then_inc(kd_in[p], 16)
                    need(sp, s["val_ok"], i + 1)
                    need(sp, s["vd_ok"], i - 1)
                    for b in range(2):
                        sp.dma_start(v_swap[(1 - b) * S:(2 - b) * S, p, :], v_s[b * S:(b + 1) * S, k, :])\
                            .then_inc(swap_in[p], 16)
            run_steps(sp, attention_moves, 0, NT)
            sp.wait_ge(s["x3_ok"], NT)
            load_expert(E - 1)
            sp.dma_start(b2_s, b2.broadcast_to([P, E * D])).then_inc(s["b2_in"], 16)

            sp.wait_ge(s["plan_ok"], 3)
            sp.wait_ge(s["pads_out"], 16)
            for r in range(4):
                sp.wait_ge(rec_out[r], arrivals(NT - 4 + r, r, 4, 16))

            def load_slot(i, k, part):
                need(sp, s["g_y"], i - 3)
                need(sp, s["g_token"], i - 3)
                at = sp.value_load(base_tab[0:1, bass.ds(i, 1)], min_val=0, max_val=E * REGION)
                sp.dma_start(slot_rec[:, k, :], routed[bass.ds(at, P), :]).then_inc(rec_in[k], 16)
                if isinstance(i, int) and i == part[1] - 1:
                    for t in range(i - 3, i + 1):
                        sp.wait_ge(y_out[t % 4], arrivals(t, t % 4, 4, 16))
            run_slots(sp, load_slot, 0, 0, used_tab)

        @block.gpsimd
        def _(pool):
            for tile, value in ((ident, 0.0), (mhalf, -0.5), (eps, LN_EPS), (ones, 1.0)):
                pool.memset(tile[:], value).then_inc(s["first_made"], 1)
            pool.wait_ge(s["first_made"], 4)
            pool.affine_select(out=ident[:, :], in_=ident[:, :], compare_op=ALU.not_equal, fill=1.0, base=0,
                               pattern=[[-1, P]], channel_multiplier=1).then_inc(s["first_made"], 1)

            def later_consts(i):
                if i < 4:
                    pool.memset(arena[:, i * 1024:(i + 1) * 1024], 0.0).then_inc(s["zeroed"], 1)
                elif i < 6:
                    half = 2 * NPAIR * VW
                    pool.memset(arena[:, 8192 + (i - 4) * half:8192 + (i - 3) * half], 0.0).then_inc(s["zeroed"], 1)
                    pool.memset((rec, pad_rec)[i - 4][:], 0.0).then_inc(s["zeroed"], 1)
                elif i == 6:
                    for tile, value in ((before16, 1.0), (zero_u, 0), (ones16, 1.0), (earlier, 1.0)):
                        pool.memset(tile[:], value).then_inc(s["consts_made"], 1)
                    pool.wait_ge(s["consts_made"], 4)
                    pool.affine_select(out=before16[:, :], in_=before16[:, :], compare_op=ALU.is_gt, fill=0.0, base=0,
                                       pattern=[[1, P]], channel_multiplier=-1).then_inc(s["consts_made"], 1)
                    pool.iota(token_ids[:, :], [[P, NT]], base=0, channel_multiplier=1).then_inc(s["consts_made"], 1)
                elif i == 7:
                    for tile, step, base, row in ((iota_e, 1, 0, 0), (region0, REGION, -P, 0), (slot_no, 0, 0, 1),
                                                  (slot_off, 0, 0, -P)):
                        pool.iota(tile[:, :], [[step, tile.shape[1]]], base=base, channel_multiplier=row,
                                  allow_small_or_imprecise_dtypes=True).then_inc(s["consts_made"], 1)
                    pool.wait_ge(s["zeroed"], ZEROED)
                    pool.iota(pad_rec[:, R_TOK:R_TOK + 1].bitcast(U32), [[0, 1]], base=NOWHERE, channel_multiplier=0)\
                        .then_inc(s["consts_made"], 1)

            def context_step(i, k):
                t, p = i + 2, k % 2
                if live(t):
                    need(pool, s["a_stats"], t + 1)
                    pool.tensor_tensor(vareps[:, p], mv[:, p, 1:2], eps[:, :], ALU.add).then_inc(s["a_vareps"], 1)
                    need(pool, s["a_vareps"], t + 1)
                    need(pool, s["a_xn"], t - 1)
                    pool.tensor_tensor(rstd[:, p], vareps[:, p], mhalf[:, :], ALU.pow).then_inc(s["a_rstd"], 1)
                u, q = i - 2, k % 2
                if live(u):
                    need(pool, s["cos_sbuf"], u + 1)
                    pool.tensor_tensor(rows(u), rows(u), cos[:, q, :], ALU.add).then_inc(s["tok_sum"], 1)
                if isinstance(i, int) and 0 <= i < LO:
                    later_consts(i)

            def attention_step(i, k):
                y, w, x, n = i - 3, i - 4, i - 6, i + 2
                if live(x):
                    need(pool, s["pos_ok"], x + 1)
                    need(pool, s["token_ok"], x + 1)
                    need(pool, s["rstd3_ok"], x + 1)
                if live(w):
                    r = (k - 4) % 4
                    need(pool, s["stats3_ok"], w + 1)
                    pool.tensor_tensor(vareps3[:, :], rec[:, r, R_VAR:R_VAR + 1], eps[:, :], ALU.add)\
                        .then_inc(s["vareps3_ok"], 1)
                    pool.tensor_copy(rec[:, r, R_TOK:R_TOK + 1].bitcast(U32), token_ids[:, bass.ds(w, 1)])\
                        .then_inc(s["token_ok"], 1)
                    need(pool, s["vareps3_ok"], w + 1)
                    pool.tensor_tensor(rec[:, r, R_RSTD:R_RSTD + 1], vareps3[:, :], mhalf[:, :], ALU.pow)\
                        .then_inc(s["rstd3_ok"], 1)
                if live(y):
                    need(pool, s["on_ok"], y + 1)
                    pool.tensor_tensor(ov[:, :], o_n[:, :], v_s[:, (k - 3) % 4, :], ALU.mult).then_inc(s["ov_ok"], 1)
                if live(i):
                    need(pool, s["xn_ok"], i + 1)
                    pool.tensor_tensor(rows(i), rows(i), bo_s[:, :], ALU.add).then_inc(s["bo_added"], 1)
                if live(y):
                    need(pool, s["coef_ok"], y + 1)
                    v_y = v_s[:, (k - 3) % 4, :].rearrange("p (h d) -> p h d", h=NH)
                    pool.tensor_tensor(along[:, :].rearrange("p (h d) -> p h d", h=NH), v_y,
                                       coef[:, :].unsqueeze(2).broadcast_to([P, NH, HD]), ALU.mult)\
                        .then_inc(s["along_ok"], 1)
                if live(x):
                    r = (k - 6) % 4
                    pool.indirect_dma_start(out=routed, out_offset=bass.IndirectOffsetOnAxis(ap=pos[:, r, :], axis=0),
                                            in_=rec[:, r, :], in_offset=None).then_inc(rec_out[r], 16)
                if live(i):
                    need(pool, s["val_ok"], i + 1)
                    need(pool, s["vvsum_raw"], i)
                    pool.tensor_tensor(vv[:, :], v_s[:, k % 4, :], v_s[:, k % 4, :], ALU.mult).then_inc(s["vv_ok"], 1)
                if live(n):
                    p = k % 2
                    need(pool, s["stats_ok"], n + 1)
                    pool.tensor_tensor(vareps[:, p], mv[:, p, 1:2], eps[:, :], ALU.add).then_inc(s["vareps_ok"], 1)
                    need(pool, s["vareps_ok"], n + 1)
                    need(pool, s["xn_ok"], n - 1)
                    pool.tensor_tensor(rstd[:, p], vareps[:, p], mhalf[:, :], ALU.pow).then_inc(s["rstd_ok"], 1)
            run_steps(pool, context_step, -2, NT - 1)
            pool.wait_ge(s["a_xn"], NT - 1)
            attention_step(-2, 2)
            context_step(NT - 1, 3)
            pool.wait_ge(s["a_xn"], NT)
            attention_step(-1, 3)
            context_step(NT, 0)
            context_step(NT + 1, 1)
            pool.wait_ge(s["consts_in"], 16 * 10)
            pool.wait_ge(s["consts_made"], CONSTS)
            run_steps(pool, attention_step, 0, NT + 6)

            def expert_step(i, k, part):
                t, r = i + 1, (k + 1) % 4
                if within(i, part):
                    need(pool, s["g_y"], i + 1)
                    need(pool, s["g_token"], i + 1)
                if within(t, part):
                    need(pool, rec_in[r], arrivals(t, r, 4, 16))
                    if not isinstance(t, int) or t >= 4:
                        need(pool, y_out[r], arrivals(t - 4, r, 4, 16))
                    pool.tensor_tensor(token_of[:, r, :], slot_rec[:, r, R_TOK:R_TOK + 1].bitcast(U32), zero_u[:, :],
                                       ALU.add).then_inc(s["g_token"], 1)
                if not within(i, part):
                    return
                pool.indirect_dma_start(
                    out=out, out_offset=bass.IndirectOffsetOnAxis(ap=token_of[:, k, :], axis=0),
                    in_=yout[:, k, :], in_offset=None, bounds_check=NTOK - 1, oob_is_err=False).then_inc(y_out[k], 16)
            run_slots(pool, expert_step, -1, 0, used_tab)

        @block.vector
        def _(dve):
            dve.wait_ge(s["first_made"], 5)

            def ones_of_values():
                dve.wait_ge(s["zeroed"], ZEROED)
                for q in range(2):
                    for b in range(2):
                        dve.memset(vd[0:S, q, b, :, HD:HD + 1], 1.0).then_inc(s["vd_ones"], 1)
                        dve.memset(vd[S:P, q, b, :, VW - 1:VW], 1.0).then_inc(s["vd_ones"], 1)
                dve.memset(ends[:, :, :], 0.0).then_inc(s["vd_ones"], 1)

            def context_step(i, k):
                t, n, u = i + 1, i + 2, i - 2
                p, q = (k + 1) % 2, k % 2
                if live(n):
                    need(dve, x_in[(k + 2) % 4], arrivals(n, (k + 2) % 4, 4, 16))
                    need(dve, s["a_vareps"], n - 1)
                    dve.bn_stats(stats[:, q, :], rows(n)).then_inc(s["a_stats_raw"], 1)
                    need(dve, s["a_stats_raw"], n + 1)
                if live(t):
                    need(dve, s["a_rstd"], t + 1)
                    need(dve, s["a_xT_psum"], t - 1)
                    dve.tensor_scalar(xn[:, p, :], rows(t), mv[:, p, 0:1], rstd[:, p], ALU.subtract, ALU.mult)\
                        .then_inc(s["a_xn"], 1)
                if live(n):
                    dve.bn_aggr(mv[:, q, :], stats[:, q, :]).then_inc(s["a_stats"], 1)
                if live(u):
                    need(dve, s["norms_sbuf"], u + 1)
                    dve.reciprocal(rnorm[:, q, :], norm[:, q, :]).then_inc(s["norms_inv"], 1)
                    need(dve, s["norms_inv"], u + 1)
                    need(dve, s["dots_psum"], u + 1)
                    need(dve, s["tok_sum"], u - 1)
                    dve.scalar_tensor_tensor(cos[:, q, :], rnorm[:, q, :], 1.0 / COS_EPS, bank(6 + q, SC),
                                             ALU.min, ALU.mult).then_inc(s["cos_sbuf"], 1)
                if isinstance(i, int) and i == HI:
                    ones_of_values()
            def attention_step(i, k):
                t, n, u, y, w, z = i + 1, i + 2, i - 1, i - 3, i - 4, i - 5
                r, zp, zr = (k - 4) % 4, (k - 5) % 2, (k - 5) % 4
                o_ps = bank(7, NH * (HD + 1)).rearrange("p (h d) -> p h d", h=NH)
                if live(w):
                    need(dve, s["wo_psum"], w + 1)
                    need(dve, s["bo_added"], w + 1)
                    if not isinstance(w, int) or w >= 4:
                        need(dve, rec_out[r], arrivals(w - 4, r, 4, 16))
                    dve.tensor_tensor(rec[:, r, 0:D], bank(6, D), rows(w), ALU.add).then_inc(s["x3_ok"], 1)
                if live(y):
                    need(dve, s["o_psum"], y + 1)
                    dve.reciprocal(rsum[:, :], o_ps[:, :, HD]).then_inc(s["rsum_ok"], 1)
                if live(w):
                    need(dve, s["x3_ok"], w + 1)
                    dve.bn_stats(stats3[:, :], rec[:, r, 0:D]).then_inc(s["stats3_raw"], 1)
                if live(z):
                    dve.max(top8[:, :], logit[:, zp, :]).then_inc(s["top_ok"], 1)
                if live(w):
                    need(dve, s["stats3_raw"], w + 1)
                if live(z):
                    need(dve, s["top_ok"], z + 1)
                    dve.tensor_scalar(ntop[:, zp, :], top8[:, 0:1], -1.0, None, ALU.mult).then_inc(s["ntop_ok"], 1)
                if live(w):
                    dve.bn_aggr(rec[:, r, R_MEAN:R_MEAN + 2], stats3[:, :]).then_inc(s["stats3_ok"], 1)
                if live(z):
                    dve.max_index(arg8[:, :], top8[:, :], logit[:, zp, :]).then_inc(s["arg_ok"], 1)
                if live(y):
                    need(dve, s["rsum_ok"], y + 1)
                    dve.tensor_tensor(o_n[:, :].rearrange("p (h d) -> p h d", h=NH), o_ps[:, :, 0:HD],
                                      rsum[:, :].unsqueeze(2).broadcast_to([P, NH, HD]), ALU.mult)\
                        .then_inc(s["on_ok"], 1)
                if live(z):
                    need(dve, s["arg_ok"], z + 1)
                    dve.tensor_copy(argf[:, zp, :], arg8[:, 0:1]).then_inc(s["argf_ok"], 1)
                if live(t):
                    p = (k + 1) % 2
                    need(dve, s["rstd_ok"], t + 1)
                    need(dve, s["xT_psum"], t - 1)
                    dve.tensor_scalar(xn[:, p, :], rows(t), mv[:, p, 0:1], rstd[:, p], ALU.subtract, ALU.mult)\
                        .then_inc(s["xn_ok"], 1)
                if live(z):
                    need(dve, s["argf_ok"], z + 1)
                    need(dve, s["rank_psum"], z - 1)
                    dve.tensor_scalar(onehot[:, zp, :], iota_e[:, :], argf[:, zp, :], None, ALU.is_equal)\
                        .then_inc(s["onehot_ok"], 1)
                if live(w):
                    need(dve, s["rstd3_ok"], w + 1)
                    need(dve, s["x3T_psum"], w - 1)
                    dve.tensor_scalar(x3n[:, k % 2, :], rec[:, r, 0:D], rec[:, r, R_MEAN:R_MEAN + 1],
                                      rec[:, r, R_RSTD:R_RSTD + 1], ALU.subtract, ALU.mult).then_inc(s["x3n_ok"], 1)
                if live(i):
                    need(dve, s["val_psum"], i + 1)
                    need(dve, s["along_ok"], i - 3)
                    dve.tensor_tensor(v_s[:, k % 4, :], bank(6, D), bv_s[:, :], ALU.add).then_inc(s["val_ok"], 1)
                if live(y):
                    need(dve, s["ov_ok"], y + 1)
                    dve.tensor_reduce(dot[:, :], ov[:, :].rearrange("p (h d) -> p h d", h=NH), AX.X, ALU.add)\
                        .then_inc(s["dot_ok"], 1)
                    need(dve, s["dot_ok"], y + 1)
                    need(dve, s["rvv_ok"], y + 1)
                    dve.tensor_tensor(coef[:, :], dot[:, :], rvv[:, (k - 3) % 4, :], ALU.mult).then_inc(s["coef_ok"], 1)
                if live(u):
                    need(dve, s["vv_ok"], u + 1)
                    dve.tensor_reduce(vvsum[:, :], vv[:, :].rearrange("p (h d) -> p h d", h=NH), AX.X, ALU.add)\
                        .then_inc(s["vvsum_raw"], 1)
                if live(n):
                    q = k % 2
                    need(dve, s["tok_sum"], n + 1)
                    need(dve, s["vareps_ok"], n - 1)
                    dve.bn_stats(stats[:, q, :], rows(n)).then_inc(s["stats_raw"], 1)
                    need(dve, s["stats_raw"], n + 1)
                if live(z):
                    need(dve, s["onehot_ok"], z + 1)
                    need(dve, s["rank_psum"], z)
                    dve.tensor_tensor(earlier[:, 1 - zp, :], earlier[:, zp, :], onehot[:, zp, :], ALU.add)\
                        .then_inc(s["earlier_ok"], 1)
                if live(n):
                    dve.bn_aggr(mv[:, q, :], stats[:, q, :]).then_inc(s["stats_ok"], 1)
                if live(y):
                    need(dve, s["along_ok"], y + 1)
                    need(dve, s["oT_psum"], y - 1)
                    dve.tensor_tensor(o_f[:, (k - 3) % 2, :], o_n[:, :], along[:, :], ALU.subtract).then_inc(s["of_ok"], 1)
                if live(z):
                    need(dve, s["rank_psum"], z + 1)
                    need(dve, s["l_psum"], w + 1, NT)
                    dve.tensor_tensor(ranked[:, :], bank(6)[:, 320:320 + E], onehot[:, zp, :], ALU.mult)\
                        .then_inc(s["ranked_ok"], 1)
                if live(w):
                    need(dve, s["l_psum"], w + 1)
                    need(dve, s["lsum_ok"], w - 1)
                    dve.tensor_copy(logit[:, k % 2, :], bank(6)[:, 352:352 + E]).then_inc(s["logit_ok"], 1)
                if live(z):
                    need(dve, s["ranked_ok"], z + 1)
                    dve.tensor_reduce(rank[:, :], ranked[:, :], AX.X, ALU.add).then_inc(s["rank_ok"], 1)
                if live(z):
                    need(dve, s["rank_ok"], z + 1)
                    dve.scalar_tensor_tensor(posf[:, :], argf[:, zp, :], float(REGION), rank[:, :], ALU.mult, ALU.add)\
                        .then_inc(s["posf_ok"], 1)
                if live(u):
                    need(dve, s["vvsum_raw"], u + 1)
                    dve.tensor_scalar(vvsum[:, :], vvsum[:, :], ATT_EPS, None, ALU.add).then_inc(s["rvv_raw"], 1)
                s_ps = psum[:, 0:NH * S].rearrange("p (h j) -> p h j", h=NH)
                if live(u):
                    need(dve, s["s_psum"], u + 1)
                    dve.tensor_reduce(smax[:, :], s_ps, AX.X, ALU.max).then_inc(s["smax_ok"], 1)
                if live(z):
                    need(dve, s["lsum_ok"], z + 1)
                    dve.reciprocal(rec[:, zr, R_PROB:R_PROB + 1], lsum[:, zp, :])
                    need(dve, s["posf_ok"], z + 1)
                    dve.tensor_copy(pos[:, zr, :], posf[:, :]).then_inc(s["pos_ok"], 1)
                if live(u):
                    need(dve, s["rvv_raw"], u + 1)
                    dve.reciprocal(rvv[:, (k - 1) % 4, :], vvsum[:, :]).then_inc(s["rvv_ok"], 1)
                if live(w):
                    need(dve, s["logit_ok"], w + 1)
                if live(u):
                    need(dve, s["smax_ok"], u + 1)
                    need(dve, s["pT_psum"], u - 1)
                    dve.tensor_tensor(prob[:, (k - 1) % 2, :].rearrange("p (h j) -> p h j", h=NH), s_ps,
                                      smax[:, :].unsqueeze(2).broadcast_to([P, NH, S]), ALU.subtract)\
                        .then_inc(s["centred"], 1)
            run_steps(dve, context_step, -2, NT - 1)
            dve.wait_ge(s["a_vareps"], NT - 1)
            attention_step(-2, 2)
            context_step(NT - 1, 3)
            dve.wait_ge(s["a_vareps"], NT)
            dve.wait_ge(s["a_xT_psum"], NT - 1)
            attention_step(-1, 3)
            context_step(NT, 0)
            context_step(NT + 1, 1)
            dve.wait_ge(s["a_xT_psum"], NT)
            dve.wait_ge(s["consts_in"], 16 * 10)
            dve.wait_ge(s["consts_made"], CONSTS)
            run_steps(dve, attention_step, 0, NT + 5)

            done = [0]

            def plan(instruction):
                done[0] += 1
                instruction.then_inc(s["plan"], 1)

            def settle():
                dve.wait_ge(s["plan"], done[0])
            dve.wait_ge(s["vd_ones"], 9)
            dve.wait_ge(s["count_psum"], 1)
            count = bank(7)[0:NSLOT, 384:384 + E]
            plan(dve.tensor_scalar(counts[:, :], count, -1.0, None, ALU.add))
            plan(dve.tensor_tensor(origin[:, 0:E], count, region0[0:NSLOT, :], ALU.add))
            plan(dve.memset(origin[:, E:E + 1], float(E * REGION + P * NSLOT)))
            settle()
            plan(dve.tensor_copy(plan_i[:, :], counts[:, :]))
            settle()
            plan(dve.tensor_scalar(plan_i[:, :], plan_i[:, :], 7, None, ALU.arith_shift_right))
            settle()
            plan(dve.tensor_copy(ends[:, 0, PAD0:], plan_i[:, :]))
            settle()
            at, reach = 0, 1
            while reach < E:
                plan(dve.tensor_tensor(ends[:, 1 - at, PAD0:], ends[:, at, PAD0:], ends[:, at, PAD0 - reach:-reach],
                                       ALU.add))
                settle()
                at, reach = 1 - at, 2 * reach
            plan(dve.scalar_tensor_tensor(origin[:, 0:E], ends[:, at, PAD0 - 1:-1], float(P), origin[:, 0:E],
                                          ALU.mult, ALU.add))
            plan(dve.tensor_scalar(passed[:, :], ends[:, at, PAD0:], slot_no[0:NSLOT, :], None, ALU.is_le))
            settle()
            plan(dve.tensor_tensor(rise[:, :], origin[:, 1:E + 1], origin[:, 0:E], ALU.subtract))
            plan(dve.tensor_reduce(slot_e[:, :], passed[:, :], AX.X, ALU.add))
            settle()
            plan(dve.tensor_tensor(risen[:, :], passed[:, :], rise[:, :], ALU.mult))
            plan(dve.tensor_scalar(slot_e[:, :], slot_e[:, :], float(E - 1), None, ALU.min))
            settle()
            plan(dve.tensor_reduce(slot_b[:, :], risen[:, :], AX.X, ALU.add))
            dve.tensor_copy(used_tab[:, :], ends[0:1, at, PAD0 + E - 1:]).then_inc(s["plan_ok"], 1)
            settle()
            plan(dve.tensor_scalar(slot_b[:, :], slot_b[:, :], origin[:, 0:1], slot_off[0:NSLOT, :], ALU.add, ALU.add))
            settle()
            dve.tensor_scalar(slot_b[:, :], slot_b[:, :], float(E * REGION), None, ALU.min)\
                .then_inc(s["columns_ok"], 1)
            dve.wait_ge(s["rows_psum"], 1)
            dve.tensor_copy(expert_tab[:, :], bank(0)[0:1, 0:NSLOT]).then_inc(s["plan_ok"], 1)
            dve.tensor_copy(base_tab[:, :], bank(0)[0:1, P:P + NSLOT]).then_inc(s["plan_ok"], 1)
            dve.wait_ge(s["plan_ok"], 3)
            dve.wait_ge(s["b2_in"], 16)

            def expert_step(i, k, part):
                t, u = i + 1, i - 1
                if within(t, part):
                    r = (k + 1) % 4
                    need(dve, rec_in[r], arrivals(t, r, 4, 16))
                    need(dve, s["g_xT_psum"], t - 1)
                    dve.tensor_scalar(xg[:, r % 2, :], slot_rec[:, r, 0:D], slot_rec[:, r, R_MEAN:R_MEAN + 1],
                                      slot_rec[:, r, R_RSTD:R_RSTD + 1], ALU.subtract, ALU.mult).then_inc(s["g_xg"], 1)
                if within(i, part):
                    need(dve, s["g_h_psum"], i + 1)
                    need(dve, s["g_hT_psum"], i - 1)
                    dve.tensor_copy(hid[:, k % 2, :], bank(k % 2)).then_inc(s["g_h"], 1)
                if within(u, part):
                    r = (k - 1) % 4
                    p = r % 2
                    e = dve.value_load(expert_tab[0:1, bass.ds(u, 1)], min_val=0, max_val=E - 1)
                    need(dve, s["g_y_psum"], u + 1)
                    dve.tensor_tensor(ysum[:, p, :], bank(2 + p, D), b2_s[:, bass.ds(e * D, D)], ALU.add)\
                        .then_inc(s["g_ysum"], 1)
                    need(dve, s["g_ysum"], u + 1)
                    if not isinstance(u, int) or u >= 4:
                        need(dve, y_out[r], arrivals(u - 4, r, 4, 16))
                    dve.scalar_tensor_tensor(yout[:, r, :], ysum[:, p, :], slot_rec[:, r, R_PROB:R_PROB + 1],
                                             slot_rec[:, r, 0:D], ALU.mult, ALU.add).then_inc(s["g_y"], 1)
            run_slots(dve, expert_step, -1, 1, used_tab)

        @block.scalar
        def _(act):
            for to, source in ((wt_s[:, :, :], wtT), (wv_s[:, :, :], wvT), (xbv_s[:, :], xbv), (xbt_s[:, :], xbt)):
                act.dma_start(to, source).then_inc(s["a_consts_in"], 16)
            act.preload_act_table(ACT.Sqrt)
            act.wait_ge(s["a_consts_in"], 64)

            def context_step(i, k):
                t, p, n, u, q = i, k % 2, i + 1, i - 1, (k - 1) % 2
                if live(t):
                    need(act, s["v_psum"], t + 1)
                    need(act, s["dots_psum"], t - 1)
                    act.activation(vsq[:, p, :], bank(1, P), ACT.Square, bias=xbv_s[:, 0:1])
                    act.activation(vT[:, p, :], bank(1, P), ACT.Identity, bias=xbv_s[:, 0:1]).then_inc(s["v_sbuf"], 1)
                if live(n):
                    need(act, s["a_xT_psum"], n + 1)
                    need(act, s["v_psum"], n - 1)
                    act.activation(xnT[:, q, :], bank(0, D), ACT.Copy).then_inc(s["a_xT"], 1)
                if live(t):
                    need(act, s["t_psum"], t + 1)
                    act.activation(tT[:, p, :], bank(2 + p), ACT.Identity, bias=xbt_s[:, 0:1])
                    act.activation(tsq[:, p, :], bank(2 + p), ACT.Square, bias=xbt_s[:, 0:1]).then_inc(s["t_sbuf"], 1)
                if live(u):
                    need(act, s["norms_psum"], u + 1)
                    need(act, s["norms_inv"], u - 1)
                    act.activation(norm[:, q, :], bank(4 + q, SC), ACT.Sqrt).then_inc(s["norms_sbuf"], 1)
                if live(t):
                    need(act, s["vnorm_psum"], t + 1)
                    act.activation(vnorm[:, p, :], bank(0)[:, 2 * P:3 * P], ACT.Copy).then_inc(s["vnorm_sbuf"], 1)
            run_steps(act, context_step, -1, NT + 1)

            def attention_step(i, k):
                p, t, u, v, y, w, z = k % 2, i + 1, i - 1, i - 2, i - 3, i - 4, i - 5
                if live(z):
                    zp = (k - 5) % 2
                    need(act, s["ntop_ok"], z + 1)
                    need(act, s["pos_ok"], z - 1)
                    act.activation(expl[:, :], logit[:, zp, :], ACT.Exp, bias=ntop[:, zp, :], accum_out=lsum[:, zp, :])\
                        .then_inc(s["lsum_ok"], 1)
                if live(i):
                    need(act, s["qk_psum"], i + 1)
                    if not isinstance(i, int) or i >= 2:
                        need(act, kd_in[p], arrivals(i - 2, p, 2, 64))
                    for c in range(KC):
                        last = act.activation(kT[:, p, c * P:(c + 1) * P], bank(4)[:, c * P:(c + 1) * P],
                                              ACT.Identity, bias=bk_s[:, c:c + 1])
                    last.then_inc(s["k_ok"], 1)
                if live(w):
                    need(act, s["x3T_psum"], w + 1)
                    need(act, s["l_psum"], w - 1)
                    act.activation(x3T[:, p, :], bank(5, D), ACT.Copy).then_inc(s["x3T_ok"], 1)
                if live(v):
                    need(act, s["pT_psum"], v + 1)
                    need(act, s["o_psum"], v - 1)
                    act.activation(probT[:, p, :], psum[:, 1024:2048], ACT.Copy).then_inc(s["pT_ok"], 1)
                if live(i):
                    need(act, s["s_psum"], i - 1)
                    for c in range(KC):
                        last = act.activation(qT[:, p, c * P:(c + 1) * P], bank(4)[:, (KC + c) * P:(KC + c + 1) * P],
                                              ACT.Identity, bias=bq_s[:, c:c + 1])
                    last.then_inc(s["q_ok"], 1)
                if live(y):
                    q = (k - 3) % 2
                    need(act, s["oT_psum"], y + 1)
                    need(act, s["wo_psum"], y - 1)
                    act.activation(oT[:, q, :], bank(5, D), ACT.Copy).then_inc(s["oT_ok"], 1)
                if live(i):
                    need(act, s["k_ok"], i + 1)
                    for h in range(0, HC, 2):
                        r = slice(h * HD, (h + 1) * HD)
                        last = act.activation(kd[r, p, :, :, h * S:(h + 1) * S],
                                              kT[r, p, :].rearrange("p (c b j) -> p c b j", c=KC, b=2), ACT.Copy)
                    last.then_inc(s["kd_ok"], 1)
                if live(t):
                    need(act, s["xT_psum"], t + 1)
                    need(act, s["val_psum"], t - 1)
                    act.activation(xnT[:, 1 - p, :], bank(5, D), ACT.Copy).then_inc(s["xT_ok"], 1)
                if live(u):
                    q = (k - 1) % 2
                    need(act, s["centred"], u + 1)
                    act.activation(prob[:, q, :], prob[:, q, :], ACT.Exp, scale=HD ** -0.5).then_inc(s["exp_ok"], 1)
                    r = (k - 1) % 4
                    need(act, swap_in[q], arrivals(u, q, 2, 32))
                    need(act, s["o_psum"], u - 1)

                    def heads(tile, odd):
                        return tile.rearrange("p (n o d) -> p n o d", n=NPAIR, o=2)[:, :, odd]
                    act.activation(vd[0:S, q, 0, :, 0:HD], heads(v_s[0:S, r, :], 0), ACT.Copy)
                    act.activation(vd[S:P, q, 0, :, HD + 1:VW - 1], heads(v_swap[S:P, q, :], 1), ACT.Copy)
                    act.activation(vd[0:S, q, 1, :, 0:HD], heads(v_swap[0:S, q, :], 0), ACT.Copy)
                    act.activation(vd[S:P, q, 1, :, HD + 1:VW - 1], heads(v_s[S:P, r, :], 1), ACT.Copy)\
                        .then_inc(s["vd_ok"], 1)
            attention_step(-1, 3)
            act.preload_act_table(ACT.Exp)
            act.wait_ge(s["consts_in"], 16 * 10)
            act.wait_ge(s["vd_ones"], 9)
            run_steps(act, attention_step, 0, NT + 5)
            act.preload_act_table(ACT.Gelu)
            act.wait_ge(s["plan_ok"], 3)

            def expert_step(i, k, part):
                t = i + 1
                if within(t, part):
                    q = (k + 1) % 2
                    need(act, s["g_xT_psum"], t + 1)
                    need(act, s["g_h_psum"], t - 1)
                    act.activation(xgT[:, q, :], bank(6 + q, D), ACT.Copy).then_inc(s["g_xT"], 1)
                if within(i, part):
                    p = k % 2
                    e = act.value_load(expert_tab[0:1, bass.ds(i, 1)], min_val=0, max_val=E - 1)
                    need(act, s["g_hT_psum"], i + 1)
                    need(act, s["g_y_psum"], i - 1)
                    for f in range(FC):
                        last = act.activation(hidT[:, p, f * P:(f + 1) * P], bank(4 + p)[:, f * P:(f + 1) * P], ACT.Gelu,
                                              bias=b1_s[:, bass.ds(e * FC + f, 1)])
                    last.then_inc(s["g_hT"], 1)
            run_slots(act, expert_step, -1, 0, used_tab)

        @block.tensor
        def _(pe):
            pe.wait_ge(s["a_consts_in"], 64)
            pe.wait_ge(s["first_made"], 5)

            def turn(tile, source, signal):
                for c in range(KC):
                    mm = pe.transpose(tile[:, c * P:(c + 1) * P], source[:, c * P:(c + 1) * P], ident[:, :])
                mm.then_inc(signal, 1)

            def context_step(i, k):
                t, p, n, u, q = i, k % 2, i + 1, i - 1, (k - 1) % 2
                if live(t):
                    need(pe, s["a_xT"], t + 1)
                    need(pe, s["v_sbuf"], t)
                    for c in range(KC):
                        mm = pe.matmul(bank(1, P), wv_s[:, c, :], xnT[:, p, c * P:(c + 1) * P], start=c == 0,
                                       stop=c == KC - 1)
                    mm.then_inc(s["v_psum"], 1)
                    need(pe, ctx_in[k], arrivals(t, k, 4, 16))
                    need(pe, s["t_sbuf"], t - 1)
                    for c in range(2):
                        mm = pe.matmul(bank(2 + p), wt_s[:, c, :], ctx_in_sb[0:CK, k, c, :], start=c == 0, stop=c == 1)
                    mm.then_inc(s["t_psum"], 1)
                if live(n):
                    need(pe, s["a_xn"], n + 1)
                    need(pe, s["vnorm_sbuf"], n - 1)
                    turn(bank(0), xn[:, q, :], s["a_xT_psum"])
                if live(u):
                    need(pe, s["t_sbuf"], u + 1)
                    need(pe, s["vnorm_sbuf"], u + 1)
                    need(pe, s["norms_sbuf"], u - 1)
                    for b in range(2):
                        h = slice(b * S, (b + 1) * S)
                        mm = pe.matmul(bank(4 + q, SC)[h, :], vnorm[:, q, h], tsq[:, q, b * SC:(b + 1) * SC],
                                       start=True, stop=True)
                    mm.then_inc(s["norms_psum"], 1)
                    need(pe, s["cos_sbuf"], u - 1)
                    for b in range(2):
                        h = slice(b * S, (b + 1) * S)
                        mm = pe.matmul(bank(6 + q, SC)[h, :], vT[:, q, h], tT[:, q, b * SC:(b + 1) * SC],
                                       start=True, stop=True)
                    mm.then_inc(s["dots_psum"], 1)
                if live(t):
                    need(pe, s["a_xT"], n + 1, NT)
                    need(pe, s["v_sbuf"], t + 1)
                    pe.matmul(bank(0)[:, 2 * P:3 * P], ones[:, :], vsq[:, p, :], start=True, stop=True)\
                        .then_inc(s["vnorm_psum"], 1)
            run_steps(pe, context_step, -1, NT + 1)
            pe.wait_ge(s["consts_in"], 16 * 10)
            pe.wait_ge(s["consts_made"], CONSTS)
            pe.wait_ge(s["norms_sbuf"], NT)

            def attention_step(i, k):
                p, t, u, v, y, w, z = k % 2, i + 1, i - 1, i - 2, i - 3, i - 4, i - 5

                def scores(c):
                    q = (k - 1) % 2
                    for b in range(2):
                        h = slice(b * S, (b + 1) * S)
                        mm = pe.matmul(bank(c)[h, :], qT[:, q, c * P + b * S:c * P + (b + 1) * S], kd[:, q, c, b, :],
                                       start=True, stop=True)
                    return mm

                def first_scores():
                    if live(u):
                        q = (k - 1) % 2
                        need(pe, kd_in[q], arrivals(u, q, 2, 64))
                        need(pe, s["q_ok"], u + 1)
                        need(pe, s["kd_ok"], u + 1)
                        need(pe, s["centred"], u)
                        scores(0)

                def second_scores():
                    if live(u):
                        scores(1).then_inc(s["s_psum"], 1)

                early = isinstance(i, int) and i == NT
                if early:
                    first_scores()
                    second_scores()
                if live(i):
                    need(pe, s["xT_ok"], i + 1)
                    need(pe, s["q_ok"], i)
                    for m, weight in enumerate((wk_s, wq_s)):
                        for c in range(KC):
                            at = (m * KC + c) * P
                            for d in range(KC):
                                mm = pe.matmul(bank(4)[:, at:at + P], weight[:, d, c * P:(c + 1) * P],
                                               xnT[:, p, d * P:(d + 1) * P], start=d == 0, stop=d == KC - 1)
                    mm.then_inc(s["qk_psum"], 1)
                if live(v):
                    need(pe, s["exp_ok"], v + 1)
                    need(pe, s["pT_ok"], v)
                    for n in range(NPAIR):
                        mm = pe.transpose(psum[:, 1024 + n * P:1024 + (n + 1) * P], prob[:, p, n * P:(n + 1) * P],
                                          ident[:, :])
                    mm.then_inc(s["pT_psum"], 1)
                if live(i):
                    need(pe, s["val_ok"], i)
                    need(pe, s["x3_ok"], i - 3)
                    for d in range(KC):
                        mm = pe.matmul(bank(6, D), xnT[:, p, d * P:(d + 1) * P], av_s[:, d, :], start=d == 0,
                                       stop=d == KC - 1)
                    mm.then_inc(s["val_psum"], 1)
                if live(w):
                    need(pe, s["x3n_ok"], w + 1)
                    need(pe, s["oT_ok"], w + 1)
                    need(pe, s["xT_ok"], i + 1, NT)
                    turn(bank(5), x3n[:, p, :], s["x3T_psum"])
                if not early:
                    first_scores()
                if live(z):
                    zp = (k - 5) % 2
                    need(pe, s["val_ok"], i + 1, NT)
                    need(pe, s["earlier_ok"], z)
                    need(pe, s["onehot_ok"], z + 1)
                    pe.matmul(bank(6)[:, 320:320 + E], before16[:, :], onehot[:, zp, :], start=True, stop=False)
                    pe.matmul(bank(6)[:, 320:320 + E], ones16[:, :], earlier[:, zp, :], start=False, stop=True)\
                        .then_inc(s["rank_psum"], 1)
                if live(w):
                    need(pe, s["x3T_ok"], w + 1)
                    need(pe, s["val_ok"], i + 1, NT)
                    for d in range(KC):
                        mm = pe.matmul(bank(6)[:, 352:352 + E], x3T[:, p, d * P:(d + 1) * P], rt_s[:, d, :],
                                       start=d == 0, stop=d == KC - 1)
                    mm.then_inc(s["l_psum"], 1)
                if not early:
                    second_scores()
                if live(y):
                    q = (k - 3) % 2
                    need(pe, s["of_ok"], y + 1)
                    need(pe, s["x3T_ok"], w + 1, NT)
                    turn(bank(5), o_f[:, q, :], s["oT_psum"])
                if live(v):
                    need(pe, s["pT_ok"], v + 1)
                    need(pe, s["vd_ok"], v + 1)
                    need(pe, s["on_ok"], v)
                    for n in range(NPAIR):
                        for b in range(2):
                            h = slice(b * S, (b + 1) * S)
                            mm = pe.matmul(bank(7)[h, n * VW:(n + 1) * VW], probT[:, p, n * P + b * S:n * P + (b + 1) * S],
                                           vd[:, p, b, n, :], start=True, stop=True)
                    mm.then_inc(s["o_psum"], 1)
                if live(t):
                    need(pe, s["xn_ok"], t + 1)
                    need(pe, s["x3T_ok"], w + 1)
                    need(pe, s["oT_ok"], y + 1)
                    turn(bank(5), xn[:, 1 - p, :], s["xT_psum"])
                if live(y):
                    need(pe, s["x3_ok"], y)
                    need(pe, s["val_ok"], i + 1, NT)
                    need(pe, s["oT_ok"], y + 1)
                    need(pe, s["logit_ok"], w + 1, NT)
                    need(pe, s["ranked_ok"], z + 1, NT)
                    for d in range(KC):
                        mm = pe.matmul(bank(6, D), oT[:, q, d * P:(d + 1) * P], wo_s[:, d, :], start=d == 0,
                                       stop=d == KC - 1)
                    mm.then_inc(s["wo_psum"], 1)
            attention_step(-1, 3)
            pe.wait_ge(s["cos_sbuf"], NT - 1)
            attention_step(0, 0)
            pe.wait_ge(s["cos_sbuf"], NT)
            run_steps(pe, attention_step, 1, NT + 5)
            pe.wait_ge(s["earlier_ok"], NT)
            pe.wait_ge(s["on_ok"], NT)
            pe.matmul(bank(7)[:, 384:384 + E], ones16[:, :], earlier[:, NT % 2, :], start=True, stop=True)\
                .then_inc(s["count_psum"], 1)
            pe.wait_ge(s["columns_ok"], 1)
            for n, column in enumerate((slot_e, slot_b)):
                mm = pe.transpose(bank(0)[0:1, n * P:n * P + NSLOT], column[:, :], ident[0:NSLOT, 0:NSLOT])
            mm.then_inc(s["rows_psum"], 1)
            pe.wait_ge(s["plan_ok"], 3)
            pe.wait_ge(s["weights_in"], 16 * (HI - LO + 4))

            def expert_step(i, k, part):
                t, p, u, q = i + 1, k % 2, i - 1, (k - 1) % 2
                if within(i, part):
                    e = pe.value_load(expert_tab[0:1, bass.ds(i, 1)], min_val=0, max_val=E - 1)
                    need(pe, s["g_xT"], i + 1)
                    need(pe, s["g_h"], i - 1)
                    for c in range(KC):
                        mm = pe.matmul(bank(p), xgT[:, p, c * P:(c + 1) * P], W[:, bass.ds(e * EW + c * F, F)],
                                       start=c == 0, stop=c == KC - 1)
                    mm.then_inc(s["g_h_psum"], 1)
                if within(u, part):
                    e = pe.value_load(expert_tab[0:1, bass.ds(u, 1)], min_val=0, max_val=E - 1)
                if within(t, part):
                    need(pe, s["g_xg"], t + 1)
                    need(pe, s["g_xT"], t - 1)
                    turn(bank(6 + (k + 1) % 2), xg[:, (k + 1) % 2, :], s["g_xT_psum"])
                if within(u, part):
                    need(pe, s["g_hT"], u + 1)
                    need(pe, s["g_ysum"], u - 1)
                    for f in range(FC):
                        mm = pe.matmul(bank(2 + q, D), hidT[:, q, f * P:(f + 1) * P],
                                       W[:, bass.ds(e * EW + KC * F + f * D, D)], start=f == 0, stop=f == FC - 1)
                    mm.then_inc(s["g_y_psum"], 1)
                if within(i, part):
                    need(pe, s["g_h"], i + 1)
                    need(pe, s["g_hT"], i - 1)
                    for f in range(FC):
                        mm = pe.transpose(bank(4 + p)[:, f * P:(f + 1) * P], hid[:, p, f * P:(f + 1) * P], ident[:, :])
                    mm.then_inc(s["g_hT_psum"], 1)
            run_slots(pe, expert_step, -1, 1, used_tab)


def rows_first(a, parts):
    n = a.shape[0] // parts
    return np.ascontiguousarray(a.reshape(parts, n, a.shape[1]).transpose(1, 0, 2))


def columns(a):
    return np.ascontiguousarray(a.reshape(-1, P).T)


def lay_out(x, ctx_768, L0_xattn_Wv, L0_xattn_bv, L0_xattn_Wt, L0_xattn_bt, L0_attn_wq, L0_attn_bq, L0_attn_wk,
            L0_attn_bk, L0_attn_wv, L0_attn_bv, L0_attn_wo, L0_attn_bo, L0_ffn_router_w, L0_ffn_w1, L0_ffn_b1,
            L0_ffn_w2, L0_ffn_b2):
    w1 = L0_ffn_w1.reshape(E, KC, P, F).transpose(0, 2, 1, 3).reshape(E, P, KC * F)
    w2 = L0_ffn_w2.reshape(E, FC, P, D).transpose(0, 2, 1, 3).reshape(E, P, FC * D)
    return {
        "x": np.ascontiguousarray(x.reshape(NTOK, D)),
        "ctxT": np.ascontiguousarray(ctx_768.reshape(NT, 2 * SC, 2, CK).transpose(0, 3, 2, 1)),
        "wvT": rows_first(L0_xattn_Wv.T, KC),
        "wtT": rows_first(L0_xattn_Wt.T, 2),
        "xbv": columns(L0_xattn_bv),
        "xbt": columns(L0_xattn_bt),
        "wqT": rows_first(L0_attn_wq.T, KC),
        "wkT": rows_first(L0_attn_wk.T, KC),
        "avT": rows_first(L0_attn_wv.T, KC),
        "woT": rows_first(L0_attn_wo.T, KC),
        "bq": columns(L0_attn_bq),
        "bk": columns(L0_attn_bk),
        "bv": np.ascontiguousarray(L0_attn_bv.reshape(1, D)),
        "bo": np.ascontiguousarray(L0_attn_bo.reshape(1, D)),
        "routerT": rows_first(L0_ffn_router_w, KC),
        "weights": np.ascontiguousarray(np.stack([w1, w2], axis=1).reshape(2 * E, P, EW // 2)),
        "b1T": np.ascontiguousarray(L0_ffn_b1.reshape(E * FC, P).T),
        "b2": np.ascontiguousarray(L0_ffn_b2.reshape(1, E * D)),
    }


def kernel(**inputs):
    import concourse.bacc as bacc
    from concourse.bass_utils import run_bass_kernel_spmd

    nc = bacc.Bacc("TRN2", target_bir_lowering=False, num_devices=1)
    arrays = lay_out(**{n: np.asarray(a) for n, a in inputs.items()})
    args = {n: nc.dram_tensor(n, a.shape, F32, kind="ExternalInput").ap() for n, a in arrays.items()}
    args["out"] = nc.dram_tensor("out", (NTOK, D), F32, kind="ExternalOutput").ap()
    build(nc, **args)
    result = run_bass_kernel_spmd(nc, [arrays], core_ids=[0])
    return result.results[0]["out"].reshape(B, S, D)
```
